# Optimizing a Trainium2 kernel written in Bass

```python
import numpy as np
import jax
import jax.numpy as jnp

def _softmax(x, axis=-1):
    return jax.nn.softmax(x, axis=axis)

def _gelu(x):
    return jax.nn.gelu(x, approximate=True)

def _silu(x):
    return jax.nn.silu(x)

def _sigmoid(x):
    return jax.nn.sigmoid(x)

def _layernorm(x, axis=-1, eps=1e-05):
    m = jnp.mean(x, axis=axis, keepdims=True)
    v = jnp.var(x, axis=axis, keepdims=True)
    return (x - m) / jnp.sqrt(v + eps)

def _scatter_add(tgt, idx, src, axis=0):
    return tgt.at[idx].add(src)

def _segment_sum(src, seg, n):
    return jax.ops.segment_sum(src, seg, n)
kernel_name = 'mk_xattn_ffn_d1_seqx_r8_0a32d9'

def setup_inputs(seed: int=0):
    np.random.seed(seed)
    _w = jnp.asarray

    def _rec_inputs():
        import jax
        import jax.numpy as jnp
        _rk = jax.random.key(seed)
        x = -0.0003929 + 0.9999 * jax.random.normal(jax.random.fold_in(_rk, 1), (16, 128, 256), jnp.float32)
        _lenS = 128 - jax.random.randint(jax.random.fold_in(_rk, 7), (16,), 0, max(1, 128 // 4) + 1, jnp.int32)
        _lenS2 = 128 - jax.random.randint(jax.random.fold_in(_rk, 8), (16,), 0, max(1, 128 // 4) + 1, jnp.int32)
        _ctx_2048P = jax.random.normal(jax.random.fold_in(_rk, 11), (16, 16, 256), jnp.float32)
        _ctx_2048c = jax.random.dirichlet(jax.random.fold_in(_rk, 511), 0.3 * jnp.ones((16,), jnp.float32), (16, 128))
        _ctx_2048t = jnp.einsum('bsk,bkd->bsd', _ctx_2048c, _ctx_2048P)
        _ctx_2048t = _ctx_2048t * jax.lax.rsqrt(jnp.mean(jnp.square(_ctx_2048t)) + 1e-12) * 0.953939
        ctx_2048 = -1.39393e-06 + 0.999914 * (_ctx_2048t + 0.3 * jax.random.normal(jax.random.fold_in(_rk, 611), (16, 128, 256), jnp.float32))
        itok_BxS_0_1023 = jax.random.randint(jax.random.fold_in(_rk, 12), (16, 128), 0, 128, jnp.int32)
        return (x, ctx_2048, itok_BxS_0_1023)
    x, ctx_2048, itok_BxS_0_1023 = _rec_inputs()

    def _L0_xattn_setup():
        import jax, jax.numpy as jnp
        import numpy as np
        B, Lq, Lk = (2, 512, 128)
        Q_DIM, KV_DIM = (256, 256)
        H, HD = (16, 128)
        KVC, QC, R = (64, 96, 64)
        LOOKBACK = 8
        NEG = -1e+30

        def _rope(x, L):
            half = x.shape[-1] // 2
            inv_freq = 1.0 / 10000.0 ** (jnp.arange(half, dtype=jnp.float32) / half)
            ang = jnp.arange(L, dtype=jnp.float32)[:, None] * inv_freq
            cos, sin = (jnp.cos(ang), jnp.sin(ang))
            x1, x2 = (x[..., :half], x[..., half:])
            return jnp.concatenate([x1 * cos - x2 * sin, x1 * sin + x2 * cos], axis=-1)
        key = jax.random.key(seed)
        ks = jax.random.split(key, 11)

        def w(k, shape, fan_in):
            return jax.random.normal(k, shape, jnp.float32) / np.sqrt(fan_in).astype(np.float32)
        return {'q': jax.random.normal(ks[0], (B, Lq, Q_DIM), jnp.float32), 'kv': jax.random.normal(ks[1], (B, Lk, KV_DIM), jnp.float32), 'seg_id': jnp.sort(jax.random.randint(ks[2], (B, Lq), 0, Lk), axis=-1), 'W_kvc': w(ks[3], (KV_DIM, KVC), KV_DIM), 'W_dq': w(ks[4], (Q_DIM, QC), Q_DIM), 'W_uq': w(ks[5], (QC, H * HD), QC), 'W_qr': w(ks[6], (QC, H * R), QC), 'W_uk': w(ks[7], (KVC, H * HD), KVC), 'W_kr': w(ks[8], (KVC, R), KVC), 'W_uv': w(ks[9], (KVC, H * HD), KVC), 'W_o': w(ks[10], (H * HD, Q_DIM), H * HD)}
    _L0_xattn_all = _L0_xattn_setup()
    _L0_xattn_in = {k: v for k, v in _L0_xattn_all.items() if k in ('W_kvc', 'W_dq', 'W_uq', 'W_qr', 'W_uk', 'W_kr', 'W_uv', 'W_o')}
    del _L0_xattn_all

    def _L0_ffn_setup():
        import jax, jax.numpy as jnp
        import numpy as np
        H = 256
        I = 96
        E = 64
        TOP_K = 8
        B, S = (1, 128)
        key = jax.random.key(seed)
        ks = jax.random.split(key, 5)
        scale = 0.02
        return {'hidden_states': jax.random.normal(ks[0], (B, S, H), dtype=jnp.float32), 'W_router': jax.random.normal(ks[1], (H, E), dtype=jnp.float32) * scale, 'W_gate': jax.random.normal(ks[2], (E, H, I), dtype=jnp.float32) * scale, 'W_up': jax.random.normal(ks[3], (E, H, I), dtype=jnp.float32) * scale, 'W_down': jax.random.normal(ks[4], (E, I, H), dtype=jnp.float32) * scale}
    _L0_ffn_all = _L0_ffn_setup()
    _L0_ffn_in = {k: v for k, v in _L0_ffn_all.items() if k in ('W_router', 'W_gate', 'W_up', 'W_down')}
    del _L0_ffn_all
    return {'x': x, 'ctx_2048': ctx_2048, 'itok_BxS_0_1023': itok_BxS_0_1023, 'L0_xattn_W_kvc': _L0_xattn_in['W_kvc'], 'L0_xattn_W_dq': _L0_xattn_in['W_dq'], 'L0_xattn_W_uq': _L0_xattn_in['W_uq'], 'L0_xattn_W_qr': _L0_xattn_in['W_qr'], 'L0_xattn_W_uk': _L0_xattn_in['W_uk'], 'L0_xattn_W_kr': _L0_xattn_in['W_kr'], 'L0_xattn_W_uv': _L0_xattn_in['W_uv'], 'L0_xattn_W_o': _L0_xattn_in['W_o'], 'L0_ffn_W_router': _L0_ffn_in['W_router'], 'L0_ffn_W_gate': _L0_ffn_in['W_gate'], 'L0_ffn_W_up': _L0_ffn_in['W_up'], 'L0_ffn_W_down': _L0_ffn_in['W_down']}

def reference(x, ctx_2048, itok_BxS_0_1023, L0_xattn_W_kvc, L0_xattn_W_dq, L0_xattn_W_uq, L0_xattn_W_qr, L0_xattn_W_uk, L0_xattn_W_kr, L0_xattn_W_uv, L0_xattn_W_o, L0_ffn_W_router, L0_ffn_W_gate, L0_ffn_W_up, L0_ffn_W_down):
    import jax
    import jax.numpy as jnp

    def _L0_xattn_ref(q, kv, seg_id, W_kvc, W_dq, W_uq, W_qr, W_uk, W_kr, W_uv, W_o):
        import jax, jax.numpy as jnp
        import numpy as np
        B, Lq, Lk = (2, 512, 128)
        Q_DIM, KV_DIM = (256, 256)
        H, HD = (16, 128)
        KVC, QC, R = (64, 96, 64)
        LOOKBACK = 8
        NEG = -1e+30

        def _rope(x, L):
            half = x.shape[-1] // 2
            inv_freq = 1.0 / 10000.0 ** (jnp.arange(half, dtype=jnp.float32) / half)
            ang = jnp.arange(L, dtype=jnp.float32)[:, None] * inv_freq
            cos, sin = (jnp.cos(ang), jnp.sin(ang))
            x1, x2 = (x[..., :half], x[..., half:])
            return jnp.concatenate([x1 * cos - x2 * sin, x1 * sin + x2 * cos], axis=-1)
        b, lq, _ = q.shape
        lk = kv.shape[1]
        kv_c = kv @ W_kvc
        q_c = q @ W_dq
        q_nope = (q_c @ W_uq).reshape(b, lq, H, HD).transpose(0, 2, 1, 3)
        q_rope = (q_c @ W_qr).reshape(b, lq, H, R).transpose(0, 2, 1, 3)
        k_nope = (kv_c @ W_uk).reshape(b, lk, H, HD)
        v = (kv_c @ W_uv).reshape(b, lk, H, HD)
        k_rope = kv_c @ W_kr
        q_rope = _rope(q_rope, lq)
        k_rope = _rope(k_rope, lk)
        scale = 1.0 / np.sqrt(HD + R).astype(np.float32)
        scores = (jnp.einsum('bhqd,bkhd->bhqk', q_nope, k_nope) + jnp.einsum('bhqr,bkr->bhqk', q_rope, k_rope)) * scale
        k_ids = jnp.arange(lk)[None, None, :]
        qs = seg_id[:, :, None]
        good = (k_ids <= qs) & (k_ids >= qs - LOOKBACK)
        scores = jnp.where(good[:, None, :, :], scores, NEG)
        attn = jax.nn.softmax(scores, axis=-1)
        out = jnp.einsum('bhqk,bkhd->bqhd', attn, v).reshape(b, lq, H * HD)
        return out @ W_o

    def _L0_ffn_ref(hidden_states, W_router, W_gate, W_up, W_down):
        import jax, jax.numpy as jnp
        import numpy as np
        H = 256
        I = 96
        E = 64
        TOP_K = 8
        B, S = (1, 128)
        b, s, h = hidden_states.shape
        x = hidden_states.reshape(-1, h)
        logits = x @ W_router
        probs = jax.nn.softmax(logits.astype(jnp.float32), axis=-1)
        top_w, top_idx = jax.lax.top_k(probs, TOP_K)
        top_w = top_w / jnp.sum(top_w, axis=-1, keepdims=True)
        top_w = top_w.astype(x.dtype)
        comb = jnp.sum(jax.nn.one_hot(top_idx, E, dtype=x.dtype) * top_w[..., None], axis=1)
        g = jnp.einsum('th,ehi->eti', x, W_gate)
        u = jnp.einsum('th,ehi->eti', x, W_up)
        hmid = jax.nn.silu(g) * u
        hmid = hmid * comb.T[:, :, None]
        out = jnp.einsum('eti,eih->th', hmid, W_down)
        return out.reshape(b, s, h)
    x = x + _L0_xattn_ref(_layernorm(x, axis=-1), ctx_2048, itok_BxS_0_1023, L0_xattn_W_kvc, L0_xattn_W_dq, L0_xattn_W_uq, L0_xattn_W_qr, L0_xattn_W_uk, L0_xattn_W_kr, L0_xattn_W_uv, L0_xattn_W_o)
    x = x + _L0_ffn_ref(_layernorm(x, axis=-1), L0_ffn_W_router, L0_ffn_W_gate, L0_ffn_W_up, L0_ffn_W_down)
    return x

_drawn_inputs = setup_inputs


def setup_inputs(seed=0):
    import zlib

    import numpy as np

    out = dict(_drawn_inputs(seed))
    spreads = {}
    factors = {'L0_ffn_W_router': 8.0, 'L0_ffn_W_gate': 8.0, 'L0_ffn_W_up': 8.0, 'L0_ffn_W_down': 8.0}
    for name, (base, spread) in spreads.items():
        noise = np.random.default_rng([zlib.crc32(name.encode()), seed]).standard_normal(out[name].shape)
        drawn = base * np.exp(spread * noise) if base else spread * noise
        out[name] = jnp.asarray(drawn.astype(out[name].dtype))
    for name, factor in factors.items():
        out[name] = (out[name] * factor).astype(out[name].dtype)
    return out
```

```python
import concourse.bass as bass
from concourse import mybir
from contextlib import ExitStack

F32 = mybir.dt.float32
BF16 = mybir.dt.bfloat16
I32 = mybir.dt.int32
ALU = mybir.AluOpType
ACT = mybir.ActivationFunctionType
AX = mybir.AxisListType

P = 128
NB = 16
D = 256
DK = D // P
NH, LAT, ROT = 16, 64, 64
QC = 96
HD = 128
HALF = ROT // 2
GH = 4
NG = NH // GH
NGROUPS = NB * NG
NE, FF, TOPK = 64, 96, 8
NTOK = NB * P
EPS = 1e-5
NEG = -1e30
LOOKBACK = 8
SCALE = float((HD + ROT) ** -0.5)
TPE = NTOK
ROW = D + NE + 4
IDC = D + NE
NCH = 4
NT = -(-((NTOK * TOPK - NE) // P + NE) // NCH) * NCH
NCASTS = 6
SPARE = NE * TPE

CONSTS = [("ident", P), ("tri", P), ("cos", ROT), ("sin", ROT), ("kidx", P), ("base1", NE),
          ("upto", NE), ("tile", 2), ("dump", 1), ("tok", 1), ("thr", 16)]
COL = {}
NCONST = 0
for _n, _w in CONSTS:
    COL[_n] = (NCONST, NCONST + _w)
    NCONST += _w


def build(nc, x, ctx, seg, consts, w_kvc, w_kvc_t, w_dq, w_uq_t, w_qr, w_uk_t, w_kr, w_uv_t, w_o,
          w_router, w_gu, w_down, out):
    rows = nc.dram_tensor("rows", (NE * TPE + P, ROW), F32)
    accs = [nc.dram_tensor(f"acc{j}", (NTOK + P, D), F32) for j in range(NCH)]
    es = ExitStack()
    with es:
        def sb(name, shape, dt=F32):
            return es.enter_context(nc.sbuf_tensor(name, shape, dt))

        def pb(name):
            return es.enter_context(nc.psum_tensor(name, [P, 512], F32))

        def sem(name):
            return es.enter_context(nc.semaphore(name))

        wgu = sb("wgu", [P, NE, DK, 2 * FF])
        wdn = sb("wdn", [P, NE, D])
        xall = sb("xall", [P, NB, D])
        cst = sb("cst", [P, NCONST])

        def const(name):
            return cst[:, COL[name][0]:COL[name][1]]

        arena = wdn[:, :, :].rearrange("p e d -> p (e d)")
        used = [0]

        def carve(n):
            used[0] += n
            assert used[0] <= NE * D
            return arena[:, used[0] - n:used[0]]

        wq = carve(NH * P)[0:QC, :].rearrange("p (h c) -> p h c", h=NH)
        wc = carve(NH // 2 * D).rearrange("p (n d) -> p n d", d=D)
        wdq = carve(DK * QC).rearrange("p (k c) -> p k c", k=DK)
        wk = carve(DK * P).rearrange("p (k c) -> p k c", k=DK)
        xn = carve(D)
        ctxb = carve(D)
        xcT = carve(4 * P).rearrange("p (k c) -> p k c", k=4)
        qcT = carve(P)[0:QC, :]
        ktok = carve(P)
        kT = carve(P)
        kval = carve(LAT + 2)
        ropet = carve(2 * GH * ROT).rearrange("p (a h c) -> p a h c", a=2, h=GH)
        kropet = carve(ROT)
        qs = carve(2 * GH * P).rearrange("p (a h c) -> p a h c", a=2, h=GH)
        qT = carve(2 * GH * P).rearrange("p (a h c) -> p a h c", a=2, h=GH)
        sm = carve(2 * GH * P).rearrange("p (a h c) -> p a h c", a=2, h=GH)
        ex = carve(2 * GH * P).rearrange("p (a h c) -> p a h c", a=2, h=GH)
        eT = carve(2 * GH * P).rearrange("p (a h c) -> p a h c", a=2, h=GH)
        zn = carve(2 * GH * LAT).rearrange("p (a h c) -> p a h c", a=2, h=GH)
        zT = carve(2 * GH * LAT).rearrange("p (a k c) -> p a k c", a=2, k=2)
        smax = carve(2 * GH).rearrange("p (a h) -> p a h", a=2)
        rsum = carve(2 * GH).rearrange("p (a h) -> p a h", a=2)
        early = wgu[:, :, :, :].rearrange("p e k f -> p (e k f)")
        wuqT = early[:, 0:NH * QC].rearrange("p (h c) -> p h c", h=NH)
        wukT = early[:, 2048:2048 + NH * LAT].rearrange("p (h c) -> p h c", h=NH)
        wuvT = early[:, 4096:4096 + NH * LAT].rearrange("p (h c) -> p h c", h=NH)
        wo = early[:, 6144:6144 + NH * D].rearrange("p (h d) -> p h d", h=NH)
        wkvcT = early[0:LAT, 12288:12288 + D]
        wkr = early[0:LAT, 12800:12800 + ROT]

        scratch = sb("scratch", [P, NCH * D])
        at = [0]

        def short(*shape):
            n = 1
            for d in shape:
                n *= d
            at[0] += n
            assert at[0] <= NCH * D
            v = scratch[:, at[0] - n:at[0]]
            return v if len(shape) == 1 else v.rearrange("p (a b) -> p a b", a=shape[0])

        yt = scratch[:, :].rearrange("p (j d) -> p j d", j=NCH)
        segi = sb("segi", [P, NB], I32)
        segf = sb("segf", [P, NB])
        seglo = sb("seglo", [P, NB])
        biast = short(2, P)
        bias = sb("bias", [P, P], BF16)
        identb = sb("identb", [P, P], BF16)
        trib = sb("trib", [P, P], BF16)
        uptob = sb("uptob", [P, NE], BF16)
        onesf = sb("onesf", [P, P])
        onesb = sb("onesb", [P, P], BF16)
        stats = short(NB, 6)
        mv = sb("mv", [P, NB, 2])
        rstd = sb("rstd", [P, NB])
        mhalf = sb("mhalf", [P, NB])
        stats2 = sb("stats2", [P, 6])
        mv2 = sb("mv2", [P, 2])
        rstd2 = sb("rstd2", [P, 1])
        wrt = sb("wrt", [P, DK, NE])
        xrow = sb("xrow", [P, ROW])
        srow = sb("srow", [P, ROW])
        x2T = short(DK, P)
        logit = short(NE)
        rest = short(NE)
        top = sb("top", [P, TOPK])
        ntop = sb("ntop", [P, 1])
        prob = short(NE)
        psel = short(NE)
        psum_ = sb("psum_", [P, 1])
        pinv = sb("pinv", [P, 1])
        chosen = sb("chosen", [P, NE], BF16)
        before = sb("before", [P, NE], BF16)
        place = short(NE)
        placem = short(NE)
        slot8 = sb("slot8", [P, TOPK])
        slots = sb("slots", [P, TOPK], I32)
        cnt = sb("cnt", [NE, 16])
        ntile = sb("ntile", [NE, 1])
        ntileb = sb("ntileb", [NE, P], BF16)
        cmp_ = sb("cmp_", [P, 2, NE])
        cmpc = sb("cmpc", [P, 2, NE])
        cum = sb("cum", [P, 3, NE])
        tmap = sb("tmap", [P, 10, 2])
        diag = sb("diag", [P, P])
        tabf = sb("tabf", [P, 3, 2, P])
        tabi = sb("tabi", [1, 3, NT], I32)
        valid = sb("valid", [P, 2, P])
        dumpt = sb("dumpt", [P, 2, P])
        xt = sb("xt", [P, NCH, ROW])
        xtT = sb("xtT", [P, 2, DK, P])
        act_ = sb("act_", [P, 2, FF])
        hid = sb("hid", [P, 2, FF])
        hidT = sb("hidT", [FF, 2, P])
        idf = sb("idf", [P, NCH])
        idt = sb("idt", [P, NCH], I32)

        pQ, pT, pE, pS, pZ, pZT, pY, pM = (pb(n) for n in ("pQ", "pT", "pE", "pS", "pZ", "pZT", "pY", "pM"))
        q4 = pQ[:, :].rearrange("p (h c) -> p h c", h=GH)
        t4 = pT[:, :].rearrange("p (h c) -> p h c", h=GH)
        e4 = pE[:, :].rearrange("p (h c) -> p h c", h=GH)
        s4 = pS[:, :].rearrange("p (h c) -> p h c", h=GH)
        z4 = pZ[:, 0:GH * (LAT + 2)].rearrange("p (h c) -> p h c", h=GH)
        zt2 = pZT[:, 0:2 * P].rearrange("p (k c) -> p k c", k=2)
        m4 = pM[:, :].rearrange("p (k c) -> p k c", k=4)

        S = {}

        def s_(name):
            if name not in S:
                S[name] = sem(name)
            return S[name]

        for n in ("ld_const ld_x ld_seg ld_w1 ld_w2 ld_ctx ld_gu ld_down "
                  "casts mhalf_set rowid_set fold_mm fold_ev fold2_mm fold2_ev prefilled zeroed fillrow_set "
                  "segf_set mv_set var_set rstd_set xn_set "
                  "inT_mm inT_ev qk_mm qc_ev k_ev krope_b ktok_set kT_mm kT_ev kval_set "
                  "bias_b bias_set "
                  "y_mm x2_set st2 mv2_set var2 rstd2_set xrow_set x2T_mm x2T_ev lg_mm lg_ev top_set rest_set ntop_set "
                  "prob_set sel_set psel_set pinv_set rank_mm place_set placem_set slot8_set slots_set "
                  "before_set srow_set sent ids_next "
                  "map_mm map_s tab_diag tab_ev tab_all "
                  "passed_pool passed_dve stored fin_set").split():
            s_(n)
        for n in ("q_mm q_lat ropeb rope_set qT_mm qT_ev s_mm max_set sub_set exp_set eT_mm eT_ev z_mm rs_set zn_set zT_mm zT_ev").split():
            S[n] = [sem(f"{n}{i}") for i in range(NG)]
        for tile_stage, group_stage in (("xtT_mm", "qT_mm"), ("xtT_ev", "qT_ev"), ("gu_mm", "s_mm"), ("silu_set", "exp_set"),
                                        ("hid_set", "sub_set"), ("hT_mm", "eT_mm"), ("hT_ev", "eT_ev"), ("dn_mm", "z_mm"),
                                        ("yt_set", "zn_set")):
            S[tile_stage] = S[group_stage]
        xt_ld = [sem(f"xt_ld{j}") for j in range(NCH)]
        added = [sem(f"added{j}") for j in range(NCH)]
        acc_ld = [sem(f"acc_ld{j}") for j in range(2)]

        block = es.enter_context(nc.Block())

        def group(b, g, lag):
            d, gg = (g - lag) // NG, (g - lag) % NG
            return (d, gg) if live(b, d) else None

        def live(b, d):
            return not isinstance(b, int) or 0 <= b + d < NB

        def at(b, d):
            return b + d if d else b

        def after(b, d):
            return at(b, d + 1)

        def need(eng, s, count):
            if isinstance(count, int) and count <= 0:
                return
            eng.wait_ge(s, count)

        def passed(eng):
            eng.sem_inc(S["passed_pool" if eng is nc.gpsimd else "passed_dve"], 1)

        def schedule(eng, step):
            for b, g in [(-1, 2), (-1, 3)] + [(b, g) for b in (0, 1, 2) for g in range(NG)]:
                step(b, g)
            with eng.Fori(3, NB - 1) as b:
                for g in range(NG):
                    step(b, g)
            for b, g in [(b, g) for b in range(NB - 1, NB + 2) for g in range(NG)]:
                step(b, g)

        NR = NT // NCH

        def tile_at(n, j, lag):
            d, jj = (j - lag) // NCH, (j - lag) % NCH
            return None if isinstance(n, int) and not 0 <= n + d < NR else (d, jj)

        def tile_done(n, d):
            return at(n, d + 1 + NB)

        def entries(eng, row, n, top_value):
            _, got = nc.values_load_multi_w_load_instructions(
                tabi[0:1, row, bass.ds(n * NCH, NCH)], engines=(eng.engine,), min_val=0, max_val=top_value,
                skip_runtime_bounds_check_because="the table's makers clamp them")
            return got

        def slots_of(eng, slot):
            slot(-1, NCH - 1)
            for j in range(NCH):
                slot(0, j)
            with eng.Fori(1, NR - 1) as n:
                for j in range(NCH):
                    slot(n, j)
            for n, j in [(NR - 1, 0), (NR - 1, 1), (NR - 1, 2), (NR - 1, 3), (NR, 0), (NR, 1)]:
                slot(n, j)

        @block.sync
        def _(sp):
            sp.dma_start(cst[:, :], consts).then_inc(S["ld_const"], 16)
            sp.dma_start(xall[:, :, :], x.rearrange("b t d -> t b d")).then_inc(S["ld_x"], 16)
            sp.dma_start(segi[:, :], seg).then_inc(S["ld_seg"], 16)
            for dst, src in ((wukT, w_uk_t), (wuqT, w_uq_t), (wkvcT, w_kvc_t), (wkr, w_kr)):
                sp.dma_start(dst, src).then_inc(S["ld_w1"], 16)
            for dst, src in ((wuvT, w_uv_t), (wo, w_o), (wdq, w_dq), (wk[:, :, 0:LAT], w_kvc),
                             (wq[:, :, LAT:P], w_qr), (wrt[:, :, :], w_router)):
                sp.dma_start(dst, src).then_inc(S["ld_w2"], 16)
            def step(b, g):
                if g == 1 or (isinstance(b, int) and b == -1 and g == 2):
                    if live(b, 1):
                        need(sp, S["inT_mm"], at(b, 1))
                        sp.dma_start(ctxb, ctx[bass.ds(at(b, 1), 1), :, :].rearrange("b t d -> (b t) d")).then_inc(S["ld_ctx"], 16)
                d = 0
                if g == 3 and live(b, d):
                    if isinstance(b, int) and b == 0:
                        sp.wait_ge(S["fold_mm"], NG + 1)
                        sp.wait_ge(S["fold2_mm"], NH // 2)
                    sp.dma_start(wgu[:, bass.ds(b * 4, 4), :, :], w_gu[:, bass.ds(b * 4, 4), :, :]).then_inc(S["ld_gu"], 16)

            schedule(sp, step)
            sp.wait_ge(S["x2_set"], NB)
            for n in range(4):
                sp.dma_start(wdn[0:FF, n * 16:n * 16 + 16, :], w_down[:, n * 16:n * 16 + 16, :]).then_inc(S["ld_down"], 16)

            sp.wait_ge(S["tab_all"], 2)
            sp.wait_ge(S["sent"], NB * TOPK * 16)

            def load_tiles(n):
                first = entries(sp, 1, n, SPARE)
                for j in range(NCH):
                    if not isinstance(n, int):
                        sp.wait_ge(S["hid_set"][j], tile_done(n, -1))
                    sp.dma_start(xt[:, j, :], rows.ap()[bass.ds(first[j], P), :]).then_inc(xt_ld[j], 16)

            load_tiles(0)
            with sp.Fori(1, NR) as n:
                load_tiles(n)

            for j in range(NCH):
                sp.wait_ge(added[j], NT // NCH * 16)
            accb = wgu[:, :, :, :].rearrange("p e k f -> p (e k f)")[:, 0:NB * NCH * D].rearrange(
                "p (a b d) -> p a b d", a=NCH, d=D)
            sp.wait_ge(S["gu_mm"][NCH - 1], tile_done(NR - 1, 0))
            for h in range(2):
                for j in range(NCH):
                    sp.dma_start(accb[:, j, h * 8:h * 8 + 8, :],
                                 accs[j].ap()[h * 8 * P:(h * 8 + 8) * P, :].rearrange("(b t) d -> t b d", t=P)).then_inc(acc_ld[h], 16)
            for h in range(2):
                sp.wait_ge(S["fin_set"], NCH * (h + 1))
                sp.dma_start(out[h * 8:h * 8 + 8].rearrange("b t d -> t b d"), xall[:, h * 8:h * 8 + 8, :]).then_inc(S["stored"], 16)
            sp.wait_ge(S["stored"], 32)

        @block.gpsimd
        def _(pool):
            nc.gpsimd.memset(onesb[:, :], 1.0).then_inc(S["casts"], 1)
            nc.gpsimd.memset(onesf[:, :], 1.0).then_inc(S["casts"], 1)
            nc.gpsimd.memset(before[:, :], 0.0).then_inc(S["before_set"], 1)
            nc.gpsimd.memset(mhalf[:, :], -0.5).then_inc(S["mhalf_set"], 1)
            nc.gpsimd.memset(kval[:, LAT:LAT + 2], 1.0).then_inc(S["casts"], 1)
            nc.gpsimd.memset(srow[:, :], 0.0).then_inc(S["fillrow_set"], 1)
            nc.gpsimd.memset(xrow[:, IDC:ROW], 0.0).then_inc(S["rowid_set"], 1)
            pool.wait_ge(S["ld_const"], 16)
            nc.gpsimd.tensor_copy(identb[:, :], const("ident")).then_inc(S["casts"], 1)
            nc.gpsimd.tensor_copy(trib[:, :], const("tri")).then_inc(S["casts"], 1)
            nc.gpsimd.tensor_copy(uptob[:, :], const("upto")).then_inc(S["casts"], 1)
            pool.wait_ge(S["fillrow_set"], 1)
            nc.gpsimd.tensor_copy(srow[:, IDC:IDC + 1], const("dump")).then_inc(S["fillrow_set"], 1)
            pool.wait_ge(S["rowid_set"], 1)
            nc.gpsimd.tensor_scalar(xrow[:, IDC:IDC + 1], const("tok"), -float(P), None, ALU.add).then_inc(S["fillrow_set"], 1)
            pool.wait_ge(S["var_set"], 1)
            nc.gpsimd.tensor_tensor(rstd[:, :], mv[:, :, 1], mhalf[:, :], ALU.pow).then_inc(S["rstd_set"], 1)
            pool.wait_ge(S["prefilled"], 5 * 16)

            def step(b, g):
                if cur := group(b, g, 0):
                    d, gg = cur
                    pool.wait_ge(S["ropeb"][gg], after(b, d))
                    nc.gpsimd.tensor_tensor(qs[:, gg % 2, :, LAT:P], ropet[:, 0], ropet[:, 1], ALU.add).then_inc(S["rope_set"][gg], 1)
                d = -1
                if g == 2 and live(b, d):
                    pool.wait_ge(S["var2"], after(b, d))
                    nc.gpsimd.tensor_tensor(rstd2[:, :], mv2[:, 1:2], mhalf[:, 0:1], ALU.pow).then_inc(S["rstd2_set"], 1)
                d = -3
                if g < 3 and live(b, d):
                    if g == 0:
                        pool.wait_ge(S["srow_set"], after(b, d))
                        pool.wait_ge(S["slots_set"], after(b, d))
                        passed(pool)
                    for k in range(3 * g, min(3 * g + 3, TOPK)):
                        nc.gpsimd.indirect_dma_start(rows.ap(), bass.IndirectOffsetOnAxis(ap=slots[:, k:k + 1], axis=0),
                                                     srow[:, :], None).then_inc(S["sent"], 16)

            schedule(pool, step)
            for g in range(3):
                step(NB + 2, g)

            def add_tile(n, j):
                pool.wait_ge(S["yt_set"][j], tile_done(n, 0))
                if not isinstance(n, int):
                    pool.wait_ge(added[j], n * 16)
                passed(pool)
                nc.gpsimd.indirect_dma_start(accs[j].ap(), bass.IndirectOffsetOnAxis(ap=idt[:, j:j + 1], axis=0),
                                             yt[:, j, :], None, compute_op=ALU.add).then_inc(added[j], 16)

            pool.wait_ge(S["zeroed"], NCH * 16)
            for j in range(NCH):
                add_tile(0, j)
            with pool.Fori(1, NT // NCH) as n:
                for j in range(NCH):
                    add_tile(n, j)

        @block.scalar
        def _(act):
            act.wait_ge(S["fillrow_set"], 3)
            for e0 in range(0, NE, 16):
                act.dma_start(rows.ap()[e0 * TPE:(e0 + 16) * TPE, :].rearrange("(e t) r -> t e r", t=TPE)[0:P],
                             srow[:, :].unsqueeze(1).to_broadcast([P, 16, ROW])).then_inc(S["prefilled"], 16)
            act.dma_start(rows.ap()[SPARE:SPARE + P, :], srow[:, :]).then_inc(S["prefilled"], 16)
            for j in range(NCH):
                act.dma_start(accs[j].ap().rearrange("(a p) d -> p a d", p=P),
                             srow[:, 0:D].unsqueeze(1).to_broadcast([P, NTOK // P + 1, D])).then_inc(S["zeroed"], 16)

            for h in range(NG):
                act.wait_ge(S["fold_mm"], h + 1)
                nc.scalar.activation(wq[:, h * GH:h * GH + GH, 0:LAT],
                                     (pQ, pT, pE, pS)[h][0:QC, 0:GH * LAT].rearrange("p (h c) -> p h c", h=GH),
                                     ACT.Copy).then_inc(S["fold_ev"], 1)
            act.wait_ge(S["fold_mm"], NG + 1)
            nc.scalar.activation(wk[:, :, LAT:P], pM[:, 0:DK * ROT].rearrange("p (k c) -> p k c", k=DK), ACT.Copy).then_inc(S["fold_ev"], 1)
            for n in range(NH // 2):
                act.wait_ge(S["fold2_mm"], n + 1)
                nc.scalar.activation(wc[:, n, :], (pZ, pZT)[n % 2][:, 0:D], ACT.Copy).then_inc(S["fold2_ev"], 1)

            def step(b, g):
                if cur := group(b, g, 3):
                    d, gg = cur
                    act.wait_ge(S["zT_mm"][gg], after(b, d))
                    nc.scalar.activation(zT[:, gg % 2], zt2, ACT.Copy).then_inc(S["zT_ev"][gg], 1)
                if cur := group(b, g, 1):
                    d, gg = cur
                    act.wait_ge(S["qT_mm"][gg], after(b, d))
                    nc.scalar.activation(qT[:, gg % 2], t4, ACT.Copy).then_inc(S["qT_ev"][gg], 1)
                if cur := group(b, g, 2):
                    d, gg = cur
                    act.wait_ge(S["eT_mm"][gg], after(b, d))
                    nc.scalar.activation(eT[:, gg % 2], e4, ACT.Copy).then_inc(S["eT_ev"][gg], 1)
                if cur := group(b, g, 0):
                    d, gg = cur
                    act.wait_ge(S["ropeb"][gg], after(b, d))
                    nc.scalar.activation(qs[:, gg % 2, :, 0:LAT], q4[:, :, 0:LAT], ACT.Copy).then_inc(S["q_lat"][gg], 1)
                d = 0
                if g == 0 and live(b, d):
                    act.wait_ge(S["kT_mm"], after(b, d))
                    nc.scalar.activation(kT, m4[:, 0, :], ACT.Copy, scale=SCALE).then_inc(S["kT_ev"], 1)
                d = -2
                if g == 0 and live(b, d):
                    act.wait_ge(S["x2T_mm"], after(b, d))
                    nc.scalar.activation(x2T, m4[:, 0:DK, :], ACT.Copy).then_inc(S["x2T_ev"], 1)
                if cur := group(b, g, 1):
                    d, gg = cur
                    act.wait_ge(S["sub_set"][gg], after(b, d))
                    nc.scalar.activation(ex[:, gg % 2], sm[:, gg % 2], ACT.Exp).then_inc(S["exp_set"][gg], 1)
                d = -2
                if g == 2 and live(b, d):
                    act.wait_ge(S["ntop_set"], after(b, d))
                    nc.scalar.activation(prob, logit, ACT.Exp, bias=ntop[:, :], scale=1.0).then_inc(S["prob_set"], 1)
                d = 1
                if g == 2 and live(b, d):
                    act.wait_ge(S["inT_mm"], after(b, d))
                    nc.scalar.activation(xcT, m4, ACT.Copy).then_inc(S["inT_ev"], 1)
                if g == 3 and live(b, d):
                    act.wait_ge(S["qk_mm"], after(b, d))
                    nc.scalar.activation(qcT, m4[0:QC, 0, :], ACT.Copy).then_inc(S["qc_ev"], 1)
                    nc.scalar.activation(ktok[:, 0:LAT], m4[:, 1, 0:LAT], ACT.Copy).then_inc(S["k_ev"], 1)

            schedule(act, step)
            def slot(n, j):
                if cur := tile_at(n, j, -1):
                    d, jj = cur
                    act.wait_ge(S["xtT_mm"][jj], tile_done(n, d))
                    nc.scalar.activation(xtT[:, jj % 2], (pQ, pT)[jj % 2][:, 0:D].rearrange("p (k c) -> p k c", k=DK), ACT.Copy).then_inc(S["xtT_ev"][jj], 1)
                if cur := tile_at(n, j, 0):
                    d, jj = cur
                    act.wait_ge(S["gu_mm"][jj], tile_done(n, d))
                    nc.scalar.activation(act_[:, jj % 2], (pE, pS)[jj % 2][:, 0:FF], ACT.Silu).then_inc(S["silu_set"][jj], 1)
                if cur := tile_at(n, j, 1):
                    d, jj = cur
                    act.wait_ge(S["hT_mm"][jj], tile_done(n, d))
                    nc.scalar.activation(hidT[:, jj % 2], (pZ, pZT)[jj % 2][0:FF, 0:P], ACT.Copy).then_inc(S["hT_ev"][jj], 1)

            slots_of(act, slot)

        @block.vector
        def _(dve):
            V = nc.vector
            dve.wait_ge(S["ld_seg"], 16)
            V.tensor_copy(segf[:, :], segi[:, :]).then_inc(S["segf_set"], 1)
            dve.wait_ge(S["segf_set"], 1)
            V.tensor_scalar(seglo[:, :], segf[:, :], -float(LOOKBACK), None, ALU.add).then_inc(S["segf_set"], 1)
            dve.wait_ge(S["ld_x"], 16)
            for b in range(NB):
                V.bn_stats(stats[:, b, :], xall[:, b, :]).then_inc(S["mv_set"], 1)
            dve.wait_ge(S["mv_set"], NB)
            for b in range(NB):
                V.bn_aggr(mv[:, b, :], stats[:, b, :]).then_inc(S["mv_set"], 1)
            dve.wait_ge(S["mv_set"], 2 * NB)
            V.tensor_scalar(mv[:, :, 1], mv[:, :, 1], EPS, None, ALU.add).then_inc(S["var_set"], 1)
            dve.wait_ge(S["segf_set"], 2)
            dve.wait_ge(S["rstd_set"], 1)
            dve.wait_ge(S["ld_const"], 16)
            dve.wait_ge(S["fillrow_set"], 3)
            dve.wait_ge(S["casts"], NCASTS)

            def step(b, g):
                if live(b, 1) and (g == 1 or (isinstance(b, int) and b == -1 and g == 2)):
                    V.tensor_scalar(xn, xall[:, bass.ds(at(b, 1), 1), :].rearrange("p b d -> p (b d)"),
                                    mv[:, bass.ds(at(b, 1), 1), 0], rstd[:, bass.ds(at(b, 1), 1)], ALU.subtract, ALU.mult).then_inc(S["xn_set"], 1)
                cosb = const("cos").unsqueeze(1).to_broadcast([P, GH, ROT])
                if cur := group(b, g, 0):
                    d, gg = cur
                    dve.wait_ge(S["q_mm"][gg], after(b, d))
                    V.tensor_tensor(ropet[:, 0], q4[:, :, LAT:P], cosb, ALU.mult)
                    for a in range(2):
                        last = V.tensor_tensor(
                            ropet[:, 1, :, a * HALF:a * HALF + HALF], q4[:, :, LAT + (1 - a) * HALF:LAT + (2 - a) * HALF],
                            const("sin")[:, a * HALF:a * HALF + HALF].unsqueeze(1).to_broadcast([P, GH, HALF]), ALU.mult)
                    last.then_inc(S["ropeb"][gg], 1)
                if cur := group(b, g, 1):
                    d, gg = cur
                    dve.wait_ge(S["s_mm"][gg], after(b, d))
                    V.tensor_reduce(smax[:, gg % 2], s4, AX.X, ALU.max).then_inc(S["max_set"][gg], 1)
                    dve.wait_ge(S["max_set"][gg], after(b, d))
                    V.tensor_tensor(sm[:, gg % 2], s4, smax[:, gg % 2].unsqueeze(2).to_broadcast([P, GH, P]),
                                    ALU.subtract).then_inc(S["sub_set"][gg], 1)
                d = 0
                if g == 0 and live(b, d):
                    V.tensor_scalar(biast[:, 0, :], const("kidx"), segf[:, bass.ds(at(b, d), 1)], NEG, ALU.is_gt, ALU.mult)
                    V.tensor_scalar(biast[:, 1, :], const("kidx"), seglo[:, bass.ds(at(b, d), 1)], NEG, ALU.is_lt, ALU.mult).then_inc(S["bias_b"], 1)
                    dve.wait_ge(S["bias_b"], after(b, d))
                    V.tensor_tensor(bias[:, :], biast[:, 0, :], biast[:, 1, :], ALU.add).then_inc(S["bias_set"], 1)
                if cur := group(b, g, 2):
                    d, gg = cur
                    dve.wait_ge(S["z_mm"][gg], after(b, d))
                    V.reciprocal(rsum[:, gg % 2], z4[:, :, LAT]).then_inc(S["rs_set"][gg], 1)
                    dve.wait_ge(S["rs_set"][gg], after(b, d))
                    V.tensor_tensor(zn[:, gg % 2], z4[:, :, 0:LAT], rsum[:, gg % 2].unsqueeze(2).to_broadcast([P, GH, LAT]),
                                    ALU.mult).then_inc(S["zn_set"][gg], 1)
                d = 0
                if g == 1 and live(b, d):
                    dve.wait_ge(S["k_ev"], after(b, d))
                    V.tensor_copy(kval[:, 0:LAT], ktok[:, 0:LAT]).then_inc(S["kval_set"], 1)
                d = -1
                if g == 2 and live(b, d):
                    dve.wait_ge(S["y_mm"], after(b, d))
                    xb = xall[:, bass.ds(at(b, d), 1), :].rearrange("p b d -> p (b d)")
                    V.tensor_tensor(xb, xb, pY[:, 0:D], ALU.add).then_inc(S["x2_set"], 1)
                    dve.wait_ge(S["x2_set"], after(b, d))
                    passed(dve)
                    V.bn_stats(stats2[:, :], xb).then_inc(S["st2"], 1)
                    dve.wait_ge(S["st2"], after(b, d))
                    passed(dve)
                    V.bn_aggr(mv2[:, :], stats2[:, :]).then_inc(S["mv2_set"], 1)
                    dve.wait_ge(S["mv2_set"], after(b, d))
                    V.tensor_scalar(mv2[:, 1:2], mv2[:, 1:2], EPS, None, ALU.add).then_inc(S["var2"], 1)
                d = -2
                if g == 1 and live(b, d):
                    dve.wait_ge(S["lg_mm"], after(b, d))
                    V.tensor_copy(logit, m4[:, 0, 0:NE]).then_inc(S["lg_ev"], 1)
                    dve.wait_ge(S["lg_ev"], after(b, d))
                    passed(dve)
                    V.max(top[:, :], logit).then_inc(S["top_set"], 1)
                    dve.wait_ge(S["top_set"], after(b, d))
                    V.tensor_scalar(ntop[:, :], top[:, 0:1], -1.0, None, ALU.mult).then_inc(S["ntop_set"], 1)
                    V.match_replace(rest, top[:, :], logit, -3.0e38).then_inc(S["rest_set"], 1)
                    dve.wait_ge(S["rest_set"], after(b, d))
                    V.tensor_tensor(chosen[:, :], logit, rest, ALU.not_equal).then_inc(S["sel_set"], 1)
                if g == 2 and live(b, d):
                    dve.wait_ge(S["prob_set"], after(b, d))
                    dve.wait_ge(S["sel_set"], after(b, d))
                    V.tensor_tensor_reduce(out=psel, in0=prob, in1=chosen[:, :], scale=1.0, scalar=0.0,
                                           op0=ALU.mult, op1=ALU.add, accum_out=psum_[:, :]).then_inc(S["psel_set"], 1)
                    dve.wait_ge(S["psel_set"], after(b, d))
                    V.reciprocal(pinv[:, :], psum_[:, :]).then_inc(S["pinv_set"], 1)
                    dve.wait_ge(S["pinv_set"], after(b, d))
                    V.tensor_scalar(xrow[:, D:D + NE], psel, pinv[:, :], None, ALU.mult)
                    V.tensor_scalar(xrow[:, IDC:IDC + 1], xrow[:, IDC:IDC + 1], float(P), None, ALU.add).then_inc(S["ids_next"], 1)
                if g == 3 and live(b, 1):
                    dve.wait_ge(S["qk_mm"], after(b, 1))
                    dve.wait_ge(S["k_ev"], after(b, 1))
                    k0 = m4[:, 1, LAT:P]
                    V.tensor_tensor(ktok[:, LAT:P], k0, const("cos"), ALU.mult)
                    V.tensor_tensor(kropet[:, 0:HALF], k0[:, HALF:ROT], const("sin")[:, 0:HALF], ALU.mult)
                    V.tensor_tensor(kropet[:, HALF:ROT], k0[:, 0:HALF], const("sin")[:, HALF:ROT], ALU.mult).then_inc(S["krope_b"], 1)
                    dve.wait_ge(S["krope_b"], after(b, 1))
                    V.tensor_tensor(ktok[:, LAT:P], ktok[:, LAT:P], kropet, ALU.add).then_inc(S["ktok_set"], 1)
                d = -2
                if g == 3 and live(b, d):
                    dve.wait_ge(S["rank_mm"], after(b, d))
                    V.tensor_tensor(place, m4[:, 2, 0:NE], const("base1"), ALU.add).then_inc(S["place_set"], 1)
                    V.tensor_tensor(before[:, :], before[:, :], chosen[:, :], ALU.add).then_inc(S["before_set"], 1)
                    dve.wait_ge(S["place_set"], after(b, d))
                    V.tensor_tensor(placem, place, chosen[:, :], ALU.mult).then_inc(S["placem_set"], 1)
                    dve.wait_ge(S["placem_set"], after(b, d))
                    passed(dve)
                    V.max(slot8[:, :], placem).then_inc(S["slot8_set"], 1)
                    dve.wait_ge(S["slot8_set"], after(b, d))
                    need(dve, S["sent"], at(b, d) * (TOPK * 16))
                    if isinstance(b, int) and b == 2:
                        dve.wait_ge(S["prefilled"], 5 * 16)
                        dve.wait_ge(S["zeroed"], NCH * 16)
                    V.tensor_scalar(slots[:, :], slot8[:, :], -1.0, None, ALU.add).then_inc(S["slots_set"], 1)
                    dve.wait_ge(S["ids_next"], after(b, d))
                    V.tensor_copy(srow[:, :], xrow[:, :]).then_inc(S["srow_set"], 1)
                d = -1
                if g == 3 and live(b, d):
                    dve.wait_ge(S["rstd2_set"], after(b, d))
                    need(dve, S["srow_set"], at(b, d))
                    V.tensor_scalar(xrow[:, 0:D], xall[:, bass.ds(at(b, d), 1), :].rearrange("p b d -> p (b d)"),
                                    mv2[:, 0:1], rstd2[:, :], ALU.subtract, ALU.mult).then_inc(S["xrow_set"], 1)

            schedule(dve, step)

            dve.wait_ge(S["map_mm"], 1)
            V.tensor_tensor(cnt[:, :], pM[0:NE, 0:1].to_broadcast([NE, 16]), const("thr")[0:NE, :], ALU.is_gt).then_inc(S["map_s"], 1)
            V.tensor_copy(cum[:, 1, :], pM[:, 128:128 + NE]).then_inc(S["map_s"], 1)
            dve.wait_ge(S["map_s"], 2)
            V.reduce_sum(ntile[:, :], cnt[:, :], AX.X).then_inc(S["map_s"], 1)
            dve.wait_ge(S["map_s"], 3)
            V.tensor_copy(ntileb[:, :], ntile[:, :].to_broadcast([NE, P])).then_inc(S["map_s"], 1)
            dve.wait_ge(S["map_mm"], 2)
            V.tensor_copy(cum[:, 0, :], pM[:, 256:256 + NE]).then_inc(S["map_s"], 1)
            dve.wait_ge(S["map_s"], 5)
            k = [5]

            def link(ins):
                k[0] += 1
                ins.then_inc(S["map_s"], 1)
                dve.wait_ge(S["map_s"], k[0])

            tile3 = const("tile").unsqueeze(2).to_broadcast([P, 2, NE])
            cum3 = cum[:, 0, :].unsqueeze(1).to_broadcast([P, 2, NE])
            n3 = cum[:, 1, :].unsqueeze(1).to_broadcast([P, 2, NE])
            link(V.tensor_tensor(cmp_[:, :, :], tile3, cum3, ALU.is_ge))
            link(V.reduce_sum(tmap[:, 0, :], cmp_[:, :, :], AX.X))
            link(V.tensor_tensor(cmpc[:, :, :], cmp_[:, :, :], cum3, ALU.mult))
            link(V.tensor_reduce(tmap[:, 1, :], cmpc[:, :, :], AX.X, ALU.max))
            link(V.tensor_scalar(tmap[:, 2, :], tmap[:, 0, :], float(TPE), 1.0, ALU.mult, ALU.add))
            link(V.tensor_tensor(cmp_[:, :, :], tmap[:, 2, :].unsqueeze(2).to_broadcast([P, 2, NE]),
                                 const("base1").unsqueeze(1).to_broadcast([P, 2, NE]), ALU.is_equal))
            link(V.tensor_tensor(cmpc[:, :, :], cmp_[:, :, :], n3, ALU.mult))
            link(V.reduce_sum(tmap[:, 3, :], cmpc[:, :, :], AX.X))
            link(V.tensor_tensor(tmap[:, 4, :], const("tile"), tmap[:, 1, :], ALU.subtract))
            link(V.tensor_scalar(tmap[:, 4, :], tmap[:, 4, :], float(P), None, ALU.mult))
            link(V.tensor_scalar(tmap[:, 5, :], tmap[:, 3, :], -float(P), 0.0, ALU.add, ALU.max))
            link(V.tensor_tensor(tmap[:, 5, :], tmap[:, 5, :], tmap[:, 4, :], ALU.min))
            link(V.tensor_tensor(tmap[:, 6, :], tmap[:, 4, :], tmap[:, 5, :], ALU.subtract))
            link(V.tensor_scalar(tmap[:, 7, :], tmap[:, 0, :], float(TPE), None, ALU.mult))
            link(V.tensor_tensor(tmap[:, 8, :], tmap[:, 7, :], tmap[:, 5, :], ALU.add))
            link(V.tensor_scalar(tmap[:, 8, :], tmap[:, 8, :], float(SPARE), None, ALU.min))
            link(V.tensor_scalar(tmap[:, 9, :], tmap[:, 0, :], float(NE - 1), None, ALU.min))
            for m, r in enumerate((9, 8, 6)):
                for c in range(2):
                    u = 2 * m + c
                    if u:
                        dve.wait_ge(S["map_mm"], u + 2)
                    V.tensor_scalar(diag[:, :], const("ident"), tmap[:, r, c:c + 1], None, ALU.mult).then_inc(S["tab_diag"], 1)
                    dve.wait_ge(S["map_mm"], u + 3)
                    V.tensor_copy(tabf[:, m, c, :], pM[:, 0:P]).then_inc(S["tab_ev"], 1)
            dve.wait_ge(S["tab_ev"], 6)
            tabr = tabf[0:1, :, :, :].rearrange("p m a c -> p m (a c)")
            V.memset(tabi[0:1, 2, 0:2], 0)
            V.tensor_copy(tabi[0:1, 2, 2:NT], tabr[:, 0, 0:NT - 2])
            V.tensor_copy(tabi[0:1, 0:2, :], tabr[:, 0:2, 0:NT]).then_inc(S["tab_all"], 1)
            dumpc = const("dump").unsqueeze(2).to_broadcast([P, 2, P])
            link(V.tensor_tensor(valid[:, :, :], const("tok").unsqueeze(2).to_broadcast([P, 2, P]), tabf[:, 2, :, :], ALU.is_ge))
            link(V.tensor_tensor(dumpt[:, :, :], valid[:, :, :], dumpc, ALU.mult))
            link(V.tensor_tensor(dumpt[:, :, :], dumpc, dumpt[:, :, :], ALU.subtract))
            V.sem_inc(S["tab_all"], 1)

            validr = valid[:, :, :].rearrange("p a c -> p (a c)")
            dumpr = dumpt[:, :, :].rearrange("p a c -> p (a c)")

            held = {}

            def slot(n, j):
                if cur := tile_at(n, j, 0):
                    d, jj = cur
                    if j == 0:
                        held["expert"] = entries(dve, 0, n, NE - 1)
                    dve.wait_ge(S["silu_set"][jj], tile_done(n, d))
                    if not isinstance(n, int) or n:
                        dve.wait_ge(S["yt_set"][jj], tile_done(n, -1))
                    V.tensor_copy(idf[:, jj:jj + 1], xt[:, jj, IDC:IDC + 1])
                    V.scalar_tensor_tensor(hid[:, jj % 2], act_[:, jj % 2], xt[:, jj, bass.ds(held["expert"][jj] + D, 1)],
                                           (pE, pS)[jj % 2][:, FF:2 * FF], ALU.mult, ALU.mult).then_inc(S["hid_set"][jj], 1)
                if cur := tile_at(n, j, 2):
                    d, jj = cur
                    need(dve, added[jj], at(n, d) * 16)
                    i = bass.ds(n * NCH + (j - 2), 1)
                    V.tensor_scalar(idt[:, jj:jj + 1], idf[:, jj:jj + 1], validr[:, i], dumpr[:, i], ALU.mult, ALU.add)
                    dve.wait_ge(S["dn_mm"][jj], tile_done(n, d))
                    V.tensor_copy(yt[:, jj, :], (pY, pM)[jj % 2][:, 0:D]).then_inc(S["yt_set"][jj], 1)

            slots_of(dve, slot)
            accb = wgu[:, :, :, :].rearrange("p e k f -> p (e k f)")[:, 0:NB * NCH * D].rearrange(
                "p (a b d) -> p a b d", a=NCH, d=D)
            for h in range(2):
                dve.wait_ge(acc_ld[h], NCH * 16)
                for j in range(NCH):
                    xh = xall[:, h * 8:h * 8 + 8, :]
                    V.tensor_tensor(xh, xh, accb[:, j, h * 8:h * 8 + 8, :], ALU.add).then_inc(S["fin_set"], 1)
                    dve.wait_ge(S["fin_set"], h * NCH + j + 1)

        @block.tensor
        def _(pe):
            T = nc.tensor
            ident = const("ident")
            pe.wait_ge(S["ld_w1"], 4 * 16)
            for h in range(NG):
                for a in range(GH):
                    last = T.matmul((pQ, pT, pE, pS)[h][0:QC, a * LAT:a * LAT + LAT], wuqT[:, h * GH + a, :], wukT[:, h * GH + a, :],
                                    start=True, stop=True)
                last.then_inc(S["fold_mm"], 1)
            for k in range(DK):
                last = T.matmul(pM[:, k * ROT:k * ROT + ROT], wkvcT[:, k * P:k * P + P], wkr, start=True, stop=True)
            last.then_inc(S["fold_mm"], 1)
            pe.wait_ge(S["ld_w2"], 6 * 16)
            for n in range(NH // 2):
                if n >= 2:
                    pe.wait_ge(S["fold2_ev"], n - 1)
                for a in range(2):
                    last = T.matmul((pZ, pZT)[n % 2][a * LAT:a * LAT + LAT, 0:D], wuvT[:, 2 * n + a, :], wo[:, 2 * n + a, :],
                                    start=True, stop=True)
                last.then_inc(S["fold2_mm"], 1)
            pe.wait_ge(S["fold_ev"], NG + 1)
            pe.wait_ge(S["fold2_ev"], NH // 2)
            pe.wait_ge(S["ld_const"], 16)
            pe.wait_ge(S["casts"], NCASTS)

            def step(b, g):
                if cur := group(b, g, 3):
                    d, gg = cur
                    pe.wait_ge(S["zn_set"][gg], after(b, d))
                    for k in range(2):
                        last = T.transpose(zt2[:, k, :], zn[:, gg % 2, 2 * k:2 * k + 2, :].rearrange("p h c -> p (h c)"), ident)
                    last.then_inc(S["zT_mm"][gg], 1)
                if cur := group(b, g, 1):
                    d, gg = cur
                    pe.wait_ge(S["q_lat"][gg], after(b, d))
                    pe.wait_ge(S["rope_set"][gg], after(b, d))
                    for a in range(GH):
                        last = T.transpose(t4[:, a, :], qs[:, gg % 2, a, :], ident)
                    last.then_inc(S["qT_mm"][gg], 1)
                if cur := group(b, g, 2):
                    d, gg = cur
                    pe.wait_ge(S["exp_set"][gg], after(b, d))
                    for a in range(GH):
                        last = T.transpose(e4[:, a, :], ex[:, gg % 2, a, :], ident)
                    last.then_inc(S["eT_mm"][gg], 1)
                if cur := group(b, g, 0):
                    d, gg = cur
                    pe.wait_ge(S["qc_ev"], after(b, d))
                    T.matmul(pQ[:, :], qcT, wq[:, gg * GH:gg * GH + GH, :].rearrange("p h c -> p (h c)"),
                             start=True, stop=True).then_inc(S["q_mm"][gg], 1)
                if cur := group(b, g, 1):
                    d, gg = cur
                    pe.wait_ge(S["qT_ev"][gg], after(b, d))
                    pe.wait_ge(S["kT_ev"], after(b, d))
                    pe.wait_ge(S["bias_set"], after(b, d))
                    T.matmul(pS[:, :], identb[:, :], bias[:, :].unsqueeze(1).to_broadcast([P, GH, P]), start=True, stop=True)
                    for a in range(GH):
                        last = T.matmul(s4[:, a, :], qT[:, gg % 2, a, :], kT, start=False, stop=True, skip_group_check=True)
                    last.then_inc(S["s_mm"][gg], 1)
                d = 0
                if g == 0 and live(b, d):
                    pe.wait_ge(S["ktok_set"], after(b, d))
                    need(pe, S["place_set"], at(b, -2))
                    T.transpose(m4[:, 0, :], ktok, ident).then_inc(S["kT_mm"], 1)
                if cur := group(b, g, 2):
                    d, gg = cur
                    pe.wait_ge(S["eT_ev"][gg], after(b, d))
                    pe.wait_ge(S["kval_set"], after(b, d))
                    for a in range(GH):
                        last = T.matmul(z4[:, a, 0:LAT + 1], eT[:, gg % 2, a, :], kval[:, 0:LAT + 1], start=True, stop=True)
                    last.then_inc(S["z_mm"][gg], 1)
                d = -2
                if g == 0 and live(b, d):
                    pe.wait_ge(S["xrow_set"], after(b, d))
                    pe.wait_ge(S["kT_ev"], min(b + 1, NB) if isinstance(b, int) else b + 1)
                    for k in range(DK):
                        last = T.transpose(m4[:, k, :], xrow[:, k * P:k * P + P], ident)
                    last.then_inc(S["x2T_mm"], 1)
                if g == 1 and live(b, d):
                    pe.wait_ge(S["x2T_ev"], after(b, d))
                    for k in range(DK):
                        last = T.matmul(m4[:, 0, 0:NE], x2T[:, k, :], wrt[:, k, :], start=(k == 0), stop=(k == DK - 1))
                    last.then_inc(S["lg_mm"], 1)
                if cur := group(b, g, 3):
                    d, gg = cur
                    pe.wait_ge(S["zT_ev"][gg], after(b, d))
                    if gg == 0:
                        need(pe, S["x2_set"], at(b, d))
                    for k in range(2):
                        last = T.matmul(pY[:, 0:D], zT[:, gg % 2, k, :], wc[:, gg * 2 + k, :],
                                        start=(gg == 0 and k == 0), stop=(gg == NG - 1 and k == 1))
                    if gg == NG - 1:
                        last.then_inc(S["y_mm"], 1)
                if g == 2 and live(b, 1):
                    pe.wait_ge(S["xn_set"], after(b, 1))
                    pe.wait_ge(S["ld_ctx"], after(b, 1) * 16)
                    need(pe, S["kT_ev"], at(b, 1))
                    need(pe, S["lg_ev"], at(b, -1))
                    for k in range(DK):
                        T.transpose(m4[:, k, :], xn[:, k * P:k * P + P], ident)
                    for k in range(DK):
                        last = T.transpose(m4[:, 2 + k, :], ctxb[:, k * P:k * P + P], ident)
                    last.then_inc(S["inT_mm"], 1)
                if g == 3 and live(b, 1):
                    pe.wait_ge(S["inT_ev"], after(b, 1))
                    for k in range(DK):
                        T.matmul(m4[0:QC, 0, :], wdq[:, k, :], xcT[:, k, :], start=(k == 0), stop=(k == DK - 1))
                    for k in range(DK):
                        last = T.matmul(m4[:, 1, :], xcT[:, 2 + k, :], wk[:, k, :], start=(k == 0), stop=(k == DK - 1))
                    last.then_inc(S["qk_mm"], 1)
                d = -2
                if g == 3 and live(b, d):
                    pe.wait_ge(S["sel_set"], after(b, d))
                    if live(b, 1):
                        pe.wait_ge(S["ktok_set"], after(b, 1))
                    T.matmul(m4[:, 2, 0:NE], trib[:, :], chosen[:, :], start=True, stop=False)
                    T.matmul(m4[:, 2, 0:NE], onesb[:, :], before[:, :], start=False, stop=True).then_inc(S["rank_mm"], 1)

            schedule(pe, step)

            pe.wait_ge(S["before_set"], NB + 1)
            pe.wait_ge(S["place_set"], NB)
            T.matmul(pM[0:NE, 0:1], before[:, :], onesb[:, 0:1], start=True, stop=True)
            T.matmul(pM[:, 128:128 + NE], onesb[:, :], before[:, :], start=True, stop=True).then_inc(S["map_mm"], 1)
            pe.wait_ge(S["map_s"], 4)
            T.matmul(pM[:, 256:256 + NE], ntileb[:, :], uptob[0:NE, :], start=True, stop=True).then_inc(S["map_mm"], 1)
            pe.wait_ge(S["map_s"], 5)
            for u in range(6):
                pe.wait_ge(S["tab_diag"], u + 1)
                if u:
                    pe.wait_ge(S["tab_ev"], u)
                T.matmul(pM[:, 0:P], onesf[:, :], diag[:, :], start=True, stop=True).then_inc(S["map_mm"], 1)
            pe.wait_ge(S["tab_ev"], 6)
            pe.wait_ge(S["tab_all"], 2)
            pe.wait_ge(S["ld_gu"], NE // 4 * 16)
            pe.wait_ge(S["ld_down"], 4 * 16)

            held = {}

            def slot(n, j):
                if j == 0:
                    if tile_at(n, j, 0):
                        held["now"] = entries(pe, 0, n, NE - 1)
                    if not isinstance(n, int) or n < NR:
                        held["before"] = entries(pe, 2, n, NE - 1)
                    else:
                        held["before"] = held["now"][2:]
                if cur := tile_at(n, j, -1):
                    d, jj = cur
                    pe.wait_ge(xt_ld[jj], after(n, d) * 16)
                    for k in range(DK):
                        last = T.transpose((pQ, pT)[jj % 2][:, k * P:k * P + P], xt[:, jj, k * P:k * P + P], ident)
                    last.then_inc(S["xtT_mm"][jj], 1)
                if cur := tile_at(n, j, 0):
                    d, jj = cur
                    e = held["now"][jj]
                    pe.wait_ge(S["xtT_ev"][jj], tile_done(n, d))
                    for k in range(DK):
                        last = T.matmul((pE, pS)[jj % 2][:, 0:2 * FF], xtT[:, jj % 2, k, :],
                                        wgu[:, bass.ds(e, 1), k, :].rearrange("p e f -> p (e f)"), start=(k == 0), stop=(k == DK - 1))
                    last.then_inc(S["gu_mm"][jj], 1)
                if cur := tile_at(n, j, 1):
                    d, jj = cur
                    pe.wait_ge(S["hid_set"][jj], tile_done(n, d))
                    T.transpose((pZ, pZT)[jj % 2][0:FF, 0:P], hid[:, jj % 2], ident).then_inc(S["hT_mm"][jj], 1)
                if cur := tile_at(n, j, 2):
                    d, jj = cur
                    e = held["before"][j]
                    pe.wait_ge(S["hT_ev"][jj], tile_done(n, d))
                    if isinstance(n, int) and n == NR and j == 1:
                        pe.wait_ge(S["yt_set"][jj - 2], tile_done(n, d))
                    T.matmul((pY, pM)[jj % 2][:, 0:D], hidT[:, jj % 2], wdn[0:FF, bass.ds(e, 1), :].rearrange("p e d -> p (e d)"),
                             start=True, stop=True).then_inc(S["dn_mm"][jj], 1)

            slots_of(pe, slot)


def table():
    import numpy as np
    c = np.zeros((P, NCONST), np.float32)
    p = np.arange(P)
    half = np.arange(HALF, dtype=np.float32) / HALF
    angle = p[:, None].astype(np.float32) * (1.0 / np.float32(10000.0) ** half).astype(np.float32)
    cos, sin = np.cos(angle), np.sin(angle)
    e = np.arange(NE)
    parts = {"ident": np.eye(P), "tri": p[:, None] < p[None, :], "cos": np.concatenate([cos, cos], 1),
             "sin": np.concatenate([-sin, sin], 1), "kidx": np.tile(p, (P, 1)), "base1": np.tile(e * TPE + 1, (P, 1)),
             "upto": p[:, None] <= e[None, :], "tile": np.stack([p, p + P], 1), "dump": NTOK + p[:, None], "tok": p[:, None],
             "thr": np.tile(np.arange(16) * P, (P, 1))}
    for n, v in parts.items():
        c[:, COL[n][0]:COL[n][1]] = v
    return c


def kernel(**inputs):
    import numpy as np
    import concourse.bacc as bacc
    from concourse.bass_utils import run_bass_kernel_spmd as run

    def w(name):
        return np.ascontiguousarray(inputs[name])

    pre, ffn = "L0_xattn_W_", "L0_ffn_W_"
    arrays = {
        "x": w("x"),
        "ctx": w("ctx_2048"),
        "seg": w("itok_BxS_0_1023").T,
        "consts": table(),
        "w_kvc": w(pre + "kvc").reshape(DK, P, LAT).transpose(1, 0, 2),
        "w_kvc_t": w(pre + "kvc").T,
        "w_dq": w(pre + "dq").reshape(DK, P, QC).transpose(1, 0, 2),
        "w_uq_t": w(pre + "uq").reshape(QC, NH, HD).transpose(2, 1, 0),
        "w_qr": w(pre + "qr").reshape(QC, NH, ROT),
        "w_uk_t": w(pre + "uk").reshape(LAT, NH, HD).transpose(2, 1, 0),
        "w_kr": w(pre + "kr"),
        "w_uv_t": w(pre + "uv").reshape(LAT, NH, HD).transpose(2, 1, 0),
        "w_o": w(pre + "o").reshape(NH, HD, D).transpose(1, 0, 2),
        "w_router": w(ffn + "router").reshape(DK, P, NE).transpose(1, 0, 2),
        "w_gu": np.concatenate([w(ffn + "gate"), w(ffn + "up")], axis=2).reshape(NE, DK, P, 2 * FF).transpose(2, 0, 1, 3),
        "w_down": w(ffn + "down").transpose(1, 0, 2),
    }
    nc = bacc.Bacc("TRN2", target_bir_lowering=False, num_devices=1)
    given, args = {}, []
    for name, a in arrays.items():
        a = np.ascontiguousarray(a)
        given["in_" + name] = a
        args.append(nc.dram_tensor("in_" + name, a.shape, mybir.dt.from_np(a.dtype), kind="ExternalInput").ap())
    args.append(nc.dram_tensor("out_0", (NB, P, D), F32, kind="ExternalOutput").ap())
    build(nc, *args)
    r = run(nc, [given], core_ids=[0])
    return r.results[0]["out_0"]
```

```python
import concourse.bass as bass
from concourse import mybir
from contextlib import ExitStack

F32 = mybir.dt.float32
BF16 = mybir.dt.bfloat16
I32 = mybir.dt.int32
ALU = mybir.AluOpType
ACT = mybir.ActivationFunctionType
AX = mybir.AxisListType

P = 128
NB = 16
D = 256
DK = D // P
NH, LAT, ROT = 16, 64, 64
QC = 96
HD = 128
HALF = ROT // 2
GH = 4
NG = NH // GH
NGROUPS = NB * NG
NE, FF, TOPK = 64, 96, 8
NTOK = NB * P
EPS = 1e-5
NEG = -1e30
LOOKBACK = 8
SCALE = float((HD + ROT) ** -0.5)
TPE = NTOK
ROW = D + NE + 4
IDC = D + NE
NCH = 4
NT = -(-((NTOK * TOPK - NE) // P + NE) // NCH) * NCH
NCASTS = 5
STATS = [(0, 1), (1, 4), (4, 8), (8, 12), (12, NB)]
SUMS = [(0, 4), (4, 8), (8, 11), (11, 13), (13, 15), (15, 16)]
FOLDS = 4
ZEROS = NCH * (NB + 1)
SPARE = NE * TPE

CONSTS = [("ident", P), ("tri", P), ("cos", ROT), ("sin", ROT), ("kidx", P), ("base1", NE),
          ("upto", NE), ("tile", 2), ("dump", 1), ("tok", 1), ("thr", 16)]
COL = {}
NCONST = 0
for _n, _w in CONSTS:
    COL[_n] = (NCONST, NCONST + _w)
    NCONST += _w


def build(nc, x, ctx, seg, consts, w_kvc, w_kvc_t, w_dq, w_uq_t, w_qr, w_uk_t, w_kr, w_uv_t, w_o,
          w_router, w_gu, w_down, out):
    rows = nc.dram_tensor("rows", (NE * TPE + P, ROW), F32)
    accs = [nc.dram_tensor(f"acc{j}", (NTOK + P, D), F32) for j in range(NCH)]
    es = ExitStack()
    with es:
        def sb(name, shape, dt=F32):
            return es.enter_context(nc.sbuf_tensor(name, shape, dt))

        def pb(name):
            return es.enter_context(nc.psum_tensor(name, [P, 512], F32))

        def sem(name):
            return es.enter_context(nc.semaphore(name))

        wgu = sb("wgu", [P, NE, DK, 2 * FF])
        wdn = sb("wdn", [P, NE, D])
        xall = sb("xall", [P, NB, D])
        cst = sb("cst", [P, NCONST])

        def const(name):
            return cst[:, COL[name][0]:COL[name][1]]

        arena = wdn[:, :, :].rearrange("p e d -> p (e d)")
        used = [0]

        def carve(n):
            used[0] += n
            assert used[0] <= NE * D
            return arena[:, NE * D - used[0]:NE * D - used[0] + n]

        srow = carve(2 * ROW).rearrange("p (a r) -> p a r", a=2)
        DOWN_LAST = (NE * D - used[0]) // D
        wc = carve(NH // 2 * D).rearrange("p (n d) -> p n d", d=D)
        wdq = carve(DK * QC).rearrange("p (k c) -> p k c", k=DK)
        wk = carve(DK * P).rearrange("p (k c) -> p k c", k=DK)
        xn = carve(D)
        ctxb = carve(D)
        xcT = carve(4 * P).rearrange("p (k c) -> p k c", k=4)
        qcT = carve(P)[0:QC, :]
        ktok = carve(P)
        kT = carve(P)
        kval = carve(LAT)
        ropet = carve(2 * GH * ROT).rearrange("p (a h c) -> p a h c", a=2, h=GH)
        kropet = carve(ROT)
        qs = carve(2 * GH * P).rearrange("p (a h c) -> p a h c", a=2, h=GH)
        qT = carve(2 * GH * P).rearrange("p (a h c) -> p a h c", a=2, h=GH)
        ex = carve(2 * GH * P).rearrange("p (a h c) -> p a h c", a=2, h=GH)
        eT = carve(2 * GH * P).rearrange("p (a h c) -> p a h c", a=2, h=GH)
        zero = carve(D)
        zT = carve(2 * GH * LAT).rearrange("p (a k c) -> p a k c", a=2, k=2)
        smin = carve(2 * GH).rearrange("p (a h) -> p a h", a=2)
        esum = carve(2 * GH).rearrange("p (a h) -> p a h", a=2)
        rsum = carve(2 * GH).rearrange("p (a h) -> p a h", a=2)
        DOWN_MID = (NE * D - used[0]) // D
        wq = carve(NH * P)[0:QC, :].rearrange("p (h c) -> p h c", h=NH)
        DOWN_FREE = (NE * D - used[0]) // D
        early = wgu[:, :, :, :].rearrange("p e k f -> p (e k f)")
        wuqT = early[:, 0:NH * QC].rearrange("p (h c) -> p h c", h=NH)
        wukT = early[:, 2048:2048 + NH * LAT].rearrange("p (h c) -> p h c", h=NH)
        wuvT = early[:, 4096:4096 + NH * LAT].rearrange("p (h c) -> p h c", h=NH)
        wo = early[:, 6144:6144 + NH * D].rearrange("p (h d) -> p h d", h=NH)
        wkvcT = early[0:LAT, 12288:12288 + D]
        wkr = early[0:LAT, 12800:12800 + ROT]

        accb = early[:, 0:NB * NCH * D].rearrange("p (a b d) -> p a b d", a=NCH, d=D)

        scratch = sb("scratch", [P, NCH * D])
        at = [0]

        def short(*shape):
            n = 1
            for d in shape:
                n *= d
            at[0] += n
            assert at[0] <= NCH * D
            v = scratch[:, at[0] - n:at[0]]
            return v if len(shape) == 1 else v.rearrange("p (a b) -> p a b", a=shape[0])

        yt = scratch[:, :].rearrange("p (j d) -> p j d", j=NCH)
        diag = scratch[:, 0:6 * P].rearrange("p (c m a) -> p c m a", c=2, m=3)
        segi = sb("segi", [P, NB], I32)
        segf = sb("segf", [P, NB])
        seglo = sb("seglo", [P, NB])
        biast = short(2, P)
        bias = sb("bias", [P, P], BF16)
        identb = sb("identb", [P, P], BF16)
        trib = sb("trib", [P, P], BF16)
        uptob = sb("uptob", [P, NE], BF16)
        onesf = sb("onesf", [P, P])
        onesb = sb("onesb", [P, P], BF16)
        stats = short(NB, 6)
        mv = sb("mv", [P, NB, 2])
        rstd = sb("rstd", [P, NB])
        mhalf = sb("mhalf", [P, NB])
        stats2 = sb("stats2", [P, 6])
        mv2 = sb("mv2", [P, 2])
        rstd2 = sb("rstd2", [P, 1])
        wrt = sb("wrt", [P, DK, NE])
        xrow = sb("xrow", [P, ROW])
        x2T = short(DK, P)
        logit = short(NE)
        rest = short(NE)
        top = sb("top", [P, TOPK])
        ntop = sb("ntop", [P, 1])
        prob = short(NE)
        psel = short(NE)
        psum_ = sb("psum_", [P, 1])
        pinv = sb("pinv", [P, 1])
        chosen = sb("chosen", [P, NE], BF16)
        before = sb("before", [P, NE], BF16)
        place = short(NE)
        placem = short(NE)
        slot8 = sb("slot8", [P, TOPK])
        slots = sb("slots", [P, 2, TOPK], I32)
        cnt = sb("cnt", [NE, 16])
        ntile = sb("ntile", [NE, 1])
        ntileb = sb("ntileb", [NE, P], BF16)
        cmp_ = sb("cmp_", [P, 2, NE])
        cmpc = sb("cmpc", [P, 2, NE])
        cum = sb("cum", [P, 3, NE])
        tmap = sb("tmap", [P, 10, 2])
        tabi = sb("tabi", [1, 2, NT + 2], I32)
        valid = sb("valid", [P, 2, P])
        dumpt = sb("dumpt", [P, 2, P])
        xt = sb("xt", [P, 2 * NCH, ROW])
        tabf = xt[:, :, :].rearrange("p j r -> p (j r)")[:, 0:6 * P].rearrange("p (m c a) -> p m c a", m=3, c=2)
        xtT = sb("xtT", [P, 2, DK, P])
        act_ = sb("act_", [P, 2, FF])
        hid = sb("hid", [P, 2, FF])
        hidT = sb("hidT", [FF, 2, P])
        idf = sb("idf", [P, NCH])
        idt = sb("idt", [P, NCH], I32)

        pQ, pT, pE, pS, pZ, pR, pY, pM = (pb(n) for n in ("pQ", "pT", "pE", "pS", "pZ", "pR", "pY", "pM"))
        q4 = pQ[:, :].rearrange("p (h c) -> p h c", h=GH)
        t4 = pT[:, :].rearrange("p (h c) -> p h c", h=GH)
        e4 = pE[:, :].rearrange("p (h c) -> p h c", h=GH)
        s4 = pS[:, :].rearrange("p (h c) -> p h c", h=GH)
        z2 = pZ[:, 0:2 * P].rearrange("p (k c) -> p k c", k=2)
        m4 = pM[:, :].rearrange("p (k c) -> p k c", k=4)
        rowT = pR[:, 0:2 * P].rearrange("p (k c) -> p k c", k=2)
        logits = pR[:, 256:256 + NE]
        ranks = pR[:, 384:384 + NE]

        S = {}

        def s_(name):
            if name not in S:
                S[name] = sem(name)
            return S[name]

        for n in ("ld_const ld_x0 ld_x1 ld_x ld_seg ld_w1 ld_w2 ld_w3 ld_ctx ld_gu ld_down "
                  "casts mhalf_set rowid_set fold_mm fold_ev fold2_mm fold2_ev prefilled zeroed fillrow_set "
                  "segf_set mv_set var_set rstd_set xn_set "
                  "inT_mm inT_ev qk_mm qc_ev k_ev krope_b ktok_set kT_mm kT_ev kval_set "
                  "bias_b bias_set "
                  "y_mm x2_set st2 mv2_set var2 rstd2_set xrow_set x2T_mm x2T_ev lg_mm lg_ev top_set rest_set ntop_set "
                  "prob_set sel_set psel_set pinv_set rank_mm place_set placem_set slot8_set slots_set "
                  "before_set srow_set sent ids_next "
                  "map_mm map_s tab_diag tab_ev tab_all "
                  "passed_pool passed_dve stored fin_set").split():
            s_(n)
        for n in ("q_mm q_lat ropeb rope_set qT_mm qT_ev s_mm min_set exp_set rs_set norm_set eT_mm eT_ev z_mm zT_ev").split():
            S[n] = [sem(f"{n}{i}") for i in range(NG)]
        for tile_stage, group_stage in (("xtT_mm", "qT_mm"), ("xtT_ev", "qT_ev"), ("gu_mm", "s_mm"), ("silu_set", "exp_set"),
                                        ("hid_set", "norm_set"), ("hT_mm", "eT_mm"), ("hT_ev", "eT_ev"), ("dn_mm", "z_mm"),
                                        ("yt_set", "min_set")):
            S[tile_stage] = S[group_stage]
        xt_ld = [sem(f"xt_ld{j}") for j in range(2 * NCH)]
        added = [sem(f"added{j}") for j in range(NCH)]
        acc_ld = [sem(f"acc_ld{j}") for j in range(len(SUMS))]

        block = es.enter_context(nc.Block())

        def group(b, g, lag):
            d, gg = (g - lag) // NG, (g - lag) % NG
            return (d, gg) if live(b, d) else None

        def live(b, d):
            return not isinstance(b, int) or 0 <= b + d < NB

        def at(b, d):
            return b + d if d else b

        def foldings(b, g):
            return {0: 0, 1: 1, 2: 2, 3: 3} if b == 0 else {}

        def own(b, d):
            return int(isinstance(b, int) and b + d == NB - 1)

        def after(b, d):
            return at(b, d + 1)

        def need(eng, s, count):
            if isinstance(count, int) and count <= 0:
                return
            eng.wait_ge(s, count)

        def passed(eng):
            eng.sem_inc(S["passed_pool" if eng is nc.gpsimd else "passed_dve"], 1)

        def schedule(eng, step):
            for b, g in [(-1, 2), (-1, 3)] + [(b, g) for b in (0, 1, 2) for g in range(NG)]:
                step(b, g)
            with eng.Fori(3, NB - 1) as b:
                for g in range(NG):
                    step(b, g)
            for b, g in [(b, g) for b in range(NB - 1, NB + 2) for g in range(NG)]:
                step(b, g)

        NR = NT // NCH

        def tile_at(n, j, lag):
            d, jj = (j - lag) // NCH, (j - lag) % NCH
            assert NR % 2 == 0
            return None if isinstance(n, int) and not 0 <= n + d < NR else (d, jj)

        def tile_done(n, d):
            return at(n, d + 1 + NB)

        def entries(eng, row, first, count, top_value):
            _, got = nc.values_load_multi_w_load_instructions(
                tabi[0:1, row, bass.ds(first, count)], engines=(eng.engine,), min_val=0, max_val=top_value,
                skip_runtime_bounds_check_because="the table's makers clamp them")
            return got

        def slots_of(eng, slot):
            slot(-2, 2 * NCH - 1)
            for j in range(2 * NCH):
                slot(0, j)
            with eng.Fori(2, NR - 3, 2) as n:
                for j in range(2 * NCH):
                    slot(n, j)
            for j in range(2 * NCH + 2):
                slot(NR - 2, j)

        @block.sync
        def _(sp):
            sp.dma_start(cst[:, :], consts).then_inc(S["ld_const"], 16)
            sp.dma_start(segi[:, :], seg).then_inc(S["ld_seg"], 16)
            sp.dma_start(xall[:, 0, :], x[0]).then_inc(S["ld_x0"], 16)
            for dst, src in ((wukT, w_uk_t), (wuqT, w_uq_t), (wkvcT, w_kvc_t), (wkr, w_kr)):
                sp.dma_start(dst, src).then_inc(S["ld_w1"], 16)
            for dst, src in ((wdq, w_dq), (wk[:, :, 0:LAT], w_kvc), (wq[:, :, LAT:P], w_qr), (wrt[:, :, :], w_router)):
                sp.dma_start(dst, src).then_inc(S["ld_w2"], 16)

            def load_down(e0, e1):
                sp.dma_start(wdn[0:FF, e0:e1, :], w_down[:, e0:e1, :]).then_inc(S["ld_down"], 16)

            def step(b, g):
                first = isinstance(b, int) and b == -1 and g == 2
                if (g == 1 or first) and live(b, 1):
                    need(sp, S["inT_mm"], at(b, 1))
                    sp.dma_start(ctxb, ctx[bass.ds(at(b, 1), 1), :, :].rearrange("b t d -> (b t) d")).then_inc(S["ld_ctx"], 16)
                if first:
                    soon = STATS[1][1]
                    sp.dma_start(xall[:, 1:soon, :], x[1:soon].rearrange("b t d -> t b d")).then_inc(S["ld_x1"], 16)
                    for dst, src in ((wuvT, w_uv_t), (wo, w_o)):
                        sp.dma_start(dst, src).then_inc(S["ld_w3"], 16)
                    sp.dma_start(xall[:, soon:NB, :], x[soon:NB].rearrange("b t d -> t b d")).then_inc(S["ld_x"], 16)
                if live(b, 0):
                    sp.wait_ge(S["q_mm"][g], after(b, 0))
                    if isinstance(b, int) and b < 2:
                        if b == 0 and g == 0:
                            sp.wait_ge(S["fillrow_set"], 4)
                            sp.dma_start(rows.ap()[SPARE:SPARE + P, :], srow[:, 0, :]).then_inc(S["prefilled"], 16)
                        e0 = (b * NG + g) * (NE // 8)
                        sp.dma_start(rows.ap()[e0 * TPE:(e0 + NE // 8) * TPE, :].rearrange("(e t) r -> t e r", t=TPE)[0:P],
                                     srow[:, 0, :].unsqueeze(1).to_broadcast([P, NE // 8, ROW])).then_inc(S["prefilled"], 16)
                    sp.dma_start(accs[g].ap()[bass.ds(b * P, P), :], zero).then_inc(S["zeroed"], 16)
                    if isinstance(b, int) and b == NB - 1:
                        sp.dma_start(accs[g].ap()[NTOK:NTOK + P, :], zero).then_inc(S["zeroed"], 16)
                if isinstance(b, int) and b == 2:
                    load_down(DOWN_FREE * g // NG, DOWN_FREE * (g + 1) // NG)
                if isinstance(b, int) and b == NB and g == 0:
                    sp.wait_ge(S["q_mm"][NG - 1], NB)
                    load_down(DOWN_FREE, DOWN_MID)
                if g == 3 and live(b, 0):
                    if isinstance(b, int) and b == 0:
                        sp.wait_ge(S["fold_mm"], NG + 1)
                        sp.wait_ge(S["fold2_mm"], FOLDS)
                    sp.dma_start(wgu[:, bass.ds(b * 4, 4), :, :], w_gu[:, bass.ds(b * 4, 4), :, :]).then_inc(S["ld_gu"], 16)

            schedule(sp, step)
            sp.wait_ge(S["zeroed"], ZEROS * 16)
            paces = [("x2_set", NB), ("xrow_set", NB), ("lg_mm", NB), ("sel_set", NB), ("slots_set", NB),
                     ("map_mm", 1), ("map_mm", 2), ("tab_diag", 1)]
            for k, (name, count) in enumerate(paces):
                sp.wait_ge(S[name], count)
                load_down(DOWN_MID + (DOWN_LAST - DOWN_MID) * k // len(paces), DOWN_MID + (DOWN_LAST - DOWN_MID) * (k + 1) // len(paces))
            sp.wait_ge(S["sent"], NB * TOPK * 16)
            load_down(DOWN_LAST, NE)

            sp.wait_ge(S["tab_all"], 2)

            def load_tiles(n):
                first = entries(sp, 1, n * NCH, 2 * NCH, SPARE)
                for j in range(2 * NCH):
                    if not isinstance(n, int):
                        sp.wait_ge(S["hid_set"][j % NCH], tile_done(n, j // NCH - 2))
                    sp.dma_start(xt[:, j, :], rows.ap()[bass.ds(first[j], P), :]).then_inc(xt_ld[j], 16)

            load_tiles(0)
            with sp.Fori(2, NR - 1, 2) as n:
                load_tiles(n)

            for j in range(NCH):
                sp.wait_ge(added[j], NR * 16)
            sp.wait_ge(S["gu_mm"][NCH - 1], tile_done(NR - 1, 0))
            for h, (b0, b1) in enumerate(SUMS):
                for j in range(NCH):
                    sp.dma_start(accb[:, j, b0:b1, :],
                                 accs[j].ap()[b0 * P:b1 * P, :].rearrange("(b t) d -> t b d", t=P)).then_inc(acc_ld[h], 16)
            for h, (b0, b1) in enumerate(SUMS):
                sp.wait_ge(S["fin_set"], NCH * (h + 1))
                sp.dma_start(out[b0:b1].rearrange("b t d -> t b d"), xall[:, b0:b1, :]).then_inc(S["stored"], 16)
            sp.wait_ge(S["stored"], len(SUMS) * 16)

        @block.gpsimd
        def _(pool):
            nc.gpsimd.memset(onesb[:, :], 1.0).then_inc(S["casts"], 1)
            nc.gpsimd.memset(onesf[:, :], 1.0).then_inc(S["casts"], 1)
            nc.gpsimd.memset(before[:, :], 0.0).then_inc(S["before_set"], 1)
            nc.gpsimd.memset(mhalf[:, :], -0.5).then_inc(S["mhalf_set"], 1)
            nc.gpsimd.memset(srow[:, 0, :], 0.0).then_inc(S["fillrow_set"], 1)
            nc.gpsimd.memset(zero, 0.0).then_inc(S["fillrow_set"], 1)
            nc.gpsimd.memset(xrow[:, IDC:ROW], 0.0).then_inc(S["rowid_set"], 1)
            pool.wait_ge(S["ld_const"], 16)
            nc.gpsimd.tensor_copy(identb[:, :], const("ident")).then_inc(S["casts"], 1)
            nc.gpsimd.tensor_copy(trib[:, :], const("tri")).then_inc(S["casts"], 1)
            nc.gpsimd.tensor_copy(uptob[:, :], const("upto")).then_inc(S["casts"], 1)
            pool.wait_ge(S["fillrow_set"], 2)
            nc.gpsimd.tensor_copy(srow[:, 0, IDC:IDC + 1], const("dump")).then_inc(S["fillrow_set"], 1)
            pool.wait_ge(S["rowid_set"], 1)
            nc.gpsimd.tensor_scalar(xrow[:, IDC:IDC + 1], const("tok"), -float(P), None, ALU.add).then_inc(S["fillrow_set"], 1)
            def rsqrt(n):
                first, end = STATS[n]
                pool.wait_ge(S["var_set"], n + 1)
                nc.gpsimd.tensor_tensor(rstd[:, first:end], mv[:, first:end, 1], mhalf[:, first:end], ALU.pow).then_inc(S["rstd_set"], 1)

            rsqrt(0)

            def step(b, g):
                if cur := group(b, g, 0):
                    d, gg = cur
                    pool.wait_ge(S["ropeb"][gg], after(b, d))
                    nc.gpsimd.tensor_tensor(qs[:, gg % 2, :, LAT:P], ropet[:, 0], ropet[:, 1], ALU.add).then_inc(S["rope_set"][gg], 1)
                if isinstance(b, int) and b == 0:
                    rsqrt(g + 1)
                d = -1
                if g == 2 and live(b, d):
                    pool.wait_ge(S["var2"], after(b, d))
                    nc.gpsimd.tensor_tensor(rstd2[:, :], mv2[:, 1:2], mhalf[:, 0:1], ALU.pow).then_inc(S["rstd2_set"], 1)
                d = -3
                if g < 2 and live(b, d):
                    a = own(b, d)
                    if g == 0:
                        pool.wait_ge(S["srow_set"], after(b, d))
                        pool.wait_ge(S["slots_set"], after(b, d))
                        passed(pool)
                    for k in range(g * TOPK // 2, (g + 1) * TOPK // 2):
                        nc.gpsimd.indirect_dma_start(rows.ap(), bass.IndirectOffsetOnAxis(ap=slots[:, a, k:k + 1], axis=0),
                                                     srow[:, a, :], None).then_inc(S["sent"], 16)

            schedule(pool, step)
            for g in range(2):
                step(NB + 2, g)

            def add_tile(n, j):
                pool.wait_ge(S["yt_set"][j % NCH], tile_done(n, j // NCH))
                if not isinstance(n, int) or j >= NCH:
                    pool.wait_ge(added[j % NCH], at(n, j // NCH) * 16)
                passed(pool)
                nc.gpsimd.indirect_dma_start(accs[j % NCH].ap(), bass.IndirectOffsetOnAxis(ap=idt[:, j % NCH:j % NCH + 1], axis=0),
                                             yt[:, j % NCH, :], None, compute_op=ALU.add).then_inc(added[j % NCH], 16)

            pool.wait_ge(S["zeroed"], ZEROS * 16)
            for j in range(2 * NCH):
                add_tile(0, j)
            with pool.Fori(2, NR - 1, 2) as n:
                for j in range(2 * NCH):
                    add_tile(n, j)

        @block.scalar
        def _(act):
            for h in range(NG):
                act.wait_ge(S["fold_mm"], h + 1)
                nc.scalar.activation(wq[:, h * GH:h * GH + GH, 0:LAT],
                                     (pQ, pT, pE, pS)[h][0:QC, 0:GH * LAT].rearrange("p (h c) -> p h c", h=GH),
                                     ACT.Copy).then_inc(S["fold_ev"], 1)
            act.wait_ge(S["fold_mm"], NG + 1)
            nc.scalar.activation(wk[:, :, LAT:P], pM[:, 0:DK * ROT].rearrange("p (k c) -> p k c", k=DK), ACT.Copy).then_inc(S["fold_ev"], 1)

            def step(b, g):
                if isinstance(b, int) and g in foldings(b, g):
                    act.wait_ge(S["fold2_mm"], foldings(b, g)[g] + 1)
                    n = 2 * foldings(b, g)[g]
                    nc.scalar.activation(wc[:, n:n + 2, :], pY[:, :].rearrange("p (n d) -> p n d", n=2), ACT.Copy).then_inc(S["fold2_ev"], 1)
                if cur := group(b, g, 3):
                    d, gg = cur
                    act.wait_ge(S["z_mm"][gg], after(b, d))
                    nc.scalar.activation(zT[:, gg % 2], z2, ACT.Copy).then_inc(S["zT_ev"][gg], 1)
                if g == 0 and live(b, 0):
                    act.wait_ge(S["kT_mm"], after(b, 0))
                    nc.scalar.activation(kT, m4[:, 0, :], ACT.Copy, scale=-SCALE).then_inc(S["kT_ev"], 1)
                if g == 0 and live(b, -2):
                    act.wait_ge(S["x2T_mm"], after(b, -2))
                    nc.scalar.activation(x2T, rowT, ACT.Copy).then_inc(S["x2T_ev"], 1)
                if cur := group(b, g, 0):
                    d, gg = cur
                    act.wait_ge(S["ropeb"][gg], after(b, d))
                    nc.scalar.activation(qs[:, gg % 2, :, 0:LAT], q4[:, :, 0:LAT], ACT.Copy).then_inc(S["q_lat"][gg], 1)
                if g == 2 and live(b, -2):
                    act.wait_ge(S["ntop_set"], after(b, -2))
                    nc.scalar.activation(prob, logit, ACT.Exp, bias=ntop[:, :], scale=1.0).then_inc(S["prob_set"], 1)
                if cur := group(b, g, 2):
                    d, gg = cur
                    act.wait_ge(S["eT_mm"][gg], after(b, d))
                    nc.scalar.activation(eT[:, gg % 2], e4, ACT.Copy).then_inc(S["eT_ev"][gg], 1)
                if g == 3 and live(b, 1):
                    act.wait_ge(S["qk_mm"], after(b, 1))
                    nc.scalar.activation(qcT, m4[0:QC, 0, :], ACT.Copy).then_inc(S["qc_ev"], 1)
                    nc.scalar.activation(ktok[:, 0:LAT], m4[:, 1, 0:LAT], ACT.Copy).then_inc(S["k_ev"], 1)
                if cur := group(b, g, 1):
                    d, gg = cur
                    act.wait_ge(S["min_set"][gg], after(b, d))
                    for a in range(GH):
                        last = nc.scalar.activation(ex[:, gg % 2, a, :], s4[:, a, :], ACT.Exp, bias=smin[:, gg % 2, a:a + 1], scale=-1.0,
                                                    accum_out=esum[:, gg % 2, a:a + 1])
                    last.then_inc(S["exp_set"][gg], 1)
                if cur := group(b, g, 0):
                    d, gg = cur
                    act.wait_ge(S["qT_mm"][gg], after(b, d))
                    nc.scalar.activation(qT[:, gg % 2], t4, ACT.Copy).then_inc(S["qT_ev"][gg], 1)
                if g == 2 and live(b, 1):
                    act.wait_ge(S["inT_mm"], after(b, 1))
                    nc.scalar.activation(xcT, m4, ACT.Copy).then_inc(S["inT_ev"], 1)

            schedule(act, step)
            def slot(n, j):
                if cur := tile_at(n, j, -1):
                    d, jj = cur
                    act.wait_ge(S["xtT_mm"][jj], tile_done(n, d))
                    nc.scalar.activation(xtT[:, jj % 2], (pQ, pT)[jj % 2][:, 0:D].rearrange("p (k c) -> p k c", k=DK), ACT.Copy).then_inc(S["xtT_ev"][jj], 1)
                if cur := tile_at(n, j, 0):
                    d, jj = cur
                    act.wait_ge(S["gu_mm"][jj], tile_done(n, d))
                    nc.scalar.activation(act_[:, jj % 2], (pE, pS)[jj % 2][:, 0:FF], ACT.Silu).then_inc(S["silu_set"][jj], 1)
                if cur := tile_at(n, j, 1):
                    d, jj = cur
                    act.wait_ge(S["hT_mm"][jj], tile_done(n, d))
                    nc.scalar.activation(hidT[:, jj % 2], (pZ, pR)[jj % 2][0:FF, 0:P], ACT.Copy).then_inc(S["hT_ev"][jj], 1)

            slots_of(act, slot)

        @block.vector
        def _(dve):
            V = nc.vector
            dve.wait_ge(S["ld_seg"], 16)
            V.tensor_copy(segf[:, :], segi[:, :]).then_inc(S["segf_set"], 1)
            dve.wait_ge(S["segf_set"], 1)
            V.tensor_scalar(seglo[:, :], segf[:, :], -float(LOOKBACK), None, ALU.add).then_inc(S["segf_set"], 1)
            def norm(b):
                V.tensor_scalar(xn, xall[:, bass.ds(b, 1), :].rearrange("p b d -> p (b d)"),
                                mv[:, bass.ds(b, 1), 0], rstd[:, bass.ds(b, 1)], ALU.subtract, ALU.mult).then_inc(S["xn_set"], 1)

            def statistics(n):
                first, end = STATS[n]
                dve.wait_ge(S[("ld_x0", "ld_x1", "ld_x", "ld_x", "ld_x")[n]], 16)
                for b in range(first, end):
                    V.bn_stats(stats[:, b, :], xall[:, b, :]).then_inc(S["mv_set"], 1)
                dve.wait_ge(S["mv_set"], first + end)
                for b in range(first, end):
                    V.bn_aggr(mv[:, b, :], stats[:, b, :]).then_inc(S["mv_set"], 1)
                dve.wait_ge(S["mv_set"], 2 * end)
                V.tensor_scalar(mv[:, first:end, 1], mv[:, first:end, 1], EPS, None, ALU.add).then_inc(S["var_set"], 1)

            statistics(0)
            dve.wait_ge(S["rstd_set"], 1)
            norm(0)
            dve.wait_ge(S["segf_set"], 2)
            dve.wait_ge(S["ld_const"], 16)
            dve.wait_ge(S["fillrow_set"], 4)
            dve.wait_ge(S["casts"], NCASTS)

            def step(b, g):
                if cur := group(b, g, 2):
                    d, gg = cur
                    dve.wait_ge(S["exp_set"][gg], after(b, d))
                    V.reciprocal(rsum[:, gg % 2], esum[:, gg % 2]).then_inc(S["rs_set"][gg], 1)
                    dve.wait_ge(S["rs_set"][gg], after(b, d))
                    V.tensor_tensor(ex[:, gg % 2], ex[:, gg % 2], rsum[:, gg % 2].unsqueeze(2).to_broadcast([P, GH, P]),
                                    ALU.mult).then_inc(S["norm_set"][gg], 1)
                cosb = const("cos").unsqueeze(1).to_broadcast([P, GH, ROT])
                if cur := group(b, g, 0):
                    d, gg = cur
                    dve.wait_ge(S["q_mm"][gg], after(b, d))
                    V.tensor_tensor(ropet[:, 0], q4[:, :, LAT:P], cosb, ALU.mult)
                    for a in range(2):
                        last = V.tensor_tensor(
                            ropet[:, 1, :, a * HALF:a * HALF + HALF], q4[:, :, LAT + (1 - a) * HALF:LAT + (2 - a) * HALF],
                            const("sin")[:, a * HALF:a * HALF + HALF].unsqueeze(1).to_broadcast([P, GH, HALF]), ALU.mult)
                    last.then_inc(S["ropeb"][gg], 1)
                if g == 1 and live(b, 1):
                    if isinstance(b, int) and b < 2:
                        dve.wait_ge(S["rstd_set"], (2, len(STATS))[b])
                    norm(at(b, 1))
                if g == 2 and live(b, -2):
                    dve.wait_ge(S["rank_mm"], after(b, -2))
                    V.tensor_tensor(place, ranks, const("base1"), ALU.add).then_inc(S["place_set"], 1)
                if cur := group(b, g, 1):
                    d, gg = cur
                    dve.wait_ge(S["s_mm"][gg], after(b, d))
                    V.tensor_reduce(smin[:, gg % 2], s4, AX.X, ALU.min).then_inc(S["min_set"][gg], 1)
                if g == 0 and live(b, 0):
                    V.tensor_scalar(biast[:, 0, :], const("kidx"), segf[:, bass.ds(at(b, 0), 1)], -NEG, ALU.is_gt, ALU.mult)
                    V.tensor_scalar(biast[:, 1, :], const("kidx"), seglo[:, bass.ds(at(b, 0), 1)], -NEG, ALU.is_lt, ALU.mult).then_inc(S["bias_b"], 1)
                    dve.wait_ge(S["bias_b"], after(b, 0))
                    V.tensor_tensor(bias[:, :], biast[:, 0, :], biast[:, 1, :], ALU.add).then_inc(S["bias_set"], 1)
                if g == 2 and live(b, 0):
                    need(dve, S["z_mm"][NG - 1], at(b, 0))
                    dve.wait_ge(S["k_ev"], after(b, 0))
                    V.tensor_copy(kval, ktok[:, 0:LAT]).then_inc(S["kval_set"], 1)
                d = -1
                if g == 2 and live(b, d):
                    dve.wait_ge(S["y_mm"], after(b, d))
                    xb = xall[:, bass.ds(at(b, d), 1), :].rearrange("p b d -> p (b d)")
                    V.tensor_tensor(xb, xb, pY[:, 0:D], ALU.add).then_inc(S["x2_set"], 1)
                    dve.wait_ge(S["x2_set"], after(b, d))
                    passed(dve)
                    V.bn_stats(stats2[:, :], xb).then_inc(S["st2"], 1)
                    dve.wait_ge(S["st2"], after(b, d))
                    passed(dve)
                    V.bn_aggr(mv2[:, :], stats2[:, :]).then_inc(S["mv2_set"], 1)
                    dve.wait_ge(S["mv2_set"], after(b, d))
                    V.tensor_scalar(mv2[:, 1:2], mv2[:, 1:2], EPS, None, ALU.add).then_inc(S["var2"], 1)
                d = -2
                if g == 1 and live(b, d):
                    dve.wait_ge(S["lg_mm"], after(b, d))
                    V.tensor_copy(logit, logits).then_inc(S["lg_ev"], 1)
                    dve.wait_ge(S["lg_ev"], after(b, d))
                    passed(dve)
                    V.max(top[:, :], logit).then_inc(S["top_set"], 1)
                    dve.wait_ge(S["top_set"], after(b, d))
                    V.tensor_scalar(ntop[:, :], top[:, 0:1], -1.0, None, ALU.mult).then_inc(S["ntop_set"], 1)
                    V.match_replace(rest, top[:, :], logit, -3.0e38).then_inc(S["rest_set"], 1)
                    dve.wait_ge(S["rest_set"], after(b, d))
                    V.tensor_tensor(chosen[:, :], logit, rest, ALU.not_equal).then_inc(S["sel_set"], 1)
                if g == 2 and live(b, d):
                    dve.wait_ge(S["prob_set"], after(b, d))
                    dve.wait_ge(S["sel_set"], after(b, d))
                    V.tensor_tensor_reduce(out=psel, in0=prob, in1=chosen[:, :], scale=1.0, scalar=0.0,
                                           op0=ALU.mult, op1=ALU.add, accum_out=psum_[:, :]).then_inc(S["psel_set"], 1)
                    dve.wait_ge(S["psel_set"], after(b, d))
                    V.reciprocal(pinv[:, :], psum_[:, :]).then_inc(S["pinv_set"], 1)
                    dve.wait_ge(S["pinv_set"], after(b, d))
                    V.tensor_scalar(xrow[:, D:D + NE], psel, pinv[:, :], None, ALU.mult)
                    V.tensor_scalar(xrow[:, IDC:IDC + 1], xrow[:, IDC:IDC + 1], float(P), None, ALU.add).then_inc(S["ids_next"], 1)
                if isinstance(b, int) and b == 0:
                    statistics(g + 1)
                d = -2
                if g == 3 and live(b, d):
                    V.tensor_tensor(before[:, :], before[:, :], chosen[:, :], ALU.add).then_inc(S["before_set"], 1)
                    dve.wait_ge(S["place_set"], after(b, d))
                    V.tensor_tensor(placem, place, chosen[:, :], ALU.mult).then_inc(S["placem_set"], 1)
                    dve.wait_ge(S["placem_set"], after(b, d))
                    passed(dve)
                    V.max(slot8[:, :], placem).then_inc(S["slot8_set"], 1)
                    dve.wait_ge(S["slot8_set"], after(b, d))
                    a = own(b, d)
                    if a == 0:
                        need(dve, S["sent"], at(b, d) * (TOPK * 16))
                    if isinstance(b, int) and b == 2:
                        dve.wait_ge(S["prefilled"], 9 * 16)
                    V.tensor_scalar(slots[:, a, :], slot8[:, :], -1.0, None, ALU.add).then_inc(S["slots_set"], 1)
                    dve.wait_ge(S["ids_next"], after(b, d))
                    V.tensor_copy(srow[:, a, :], xrow[:, :]).then_inc(S["srow_set"], 1)
                d = -1
                if g == 3 and live(b, d):
                    dve.wait_ge(S["rstd2_set"], after(b, d))
                    need(dve, S["srow_set"], at(b, d))
                    V.tensor_scalar(xrow[:, 0:D], xall[:, bass.ds(at(b, d), 1), :].rearrange("p b d -> p (b d)"),
                                    mv2[:, 0:1], rstd2[:, :], ALU.subtract, ALU.mult).then_inc(S["xrow_set"], 1)
                if g == 3 and live(b, 1):
                    dve.wait_ge(S["qk_mm"], after(b, 1))
                    dve.wait_ge(S["k_ev"], after(b, 1))
                    k0 = m4[:, 1, LAT:P]
                    V.tensor_tensor(ktok[:, LAT:P], k0, const("cos"), ALU.mult)
                    V.tensor_tensor(kropet[:, 0:HALF], k0[:, HALF:ROT], const("sin")[:, 0:HALF], ALU.mult)
                    V.tensor_tensor(kropet[:, HALF:ROT], k0[:, 0:HALF], const("sin")[:, HALF:ROT], ALU.mult).then_inc(S["krope_b"], 1)
                    dve.wait_ge(S["krope_b"], after(b, 1))
                    V.tensor_tensor(ktok[:, LAT:P], ktok[:, LAT:P], kropet, ALU.add).then_inc(S["ktok_set"], 1)

            schedule(dve, step)

            dve.wait_ge(S["map_mm"], 1)
            V.tensor_tensor(cnt[:, :], pM[0:NE, 0:1].to_broadcast([NE, 16]), const("thr")[0:NE, :], ALU.is_gt).then_inc(S["map_s"], 1)
            V.tensor_copy(cum[:, 1, :], pM[:, 128:128 + NE]).then_inc(S["map_s"], 1)
            dve.wait_ge(S["map_s"], 2)
            V.reduce_sum(ntile[:, :], cnt[:, :], AX.X).then_inc(S["map_s"], 1)
            dve.wait_ge(S["map_s"], 3)
            V.tensor_copy(ntileb[:, :], ntile[:, :].to_broadcast([NE, P])).then_inc(S["map_s"], 1)
            dve.wait_ge(S["map_mm"], 2)
            V.tensor_copy(cum[:, 0, :], pM[:, 256:256 + NE]).then_inc(S["map_s"], 1)
            dve.wait_ge(S["map_s"], 5)
            k = [5]

            def link(ins):
                k[0] += 1
                ins.then_inc(S["map_s"], 1)
                dve.wait_ge(S["map_s"], k[0])

            tile3 = const("tile").unsqueeze(2).to_broadcast([P, 2, NE])
            cum3 = cum[:, 0, :].unsqueeze(1).to_broadcast([P, 2, NE])
            n3 = cum[:, 1, :].unsqueeze(1).to_broadcast([P, 2, NE])
            link(V.tensor_tensor(cmp_[:, :, :], tile3, cum3, ALU.is_ge))
            link(V.reduce_sum(tmap[:, 0, :], cmp_[:, :, :], AX.X))
            link(V.tensor_tensor(cmpc[:, :, :], cmp_[:, :, :], cum3, ALU.mult))
            link(V.tensor_reduce(tmap[:, 1, :], cmpc[:, :, :], AX.X, ALU.max))
            link(V.tensor_scalar(tmap[:, 2, :], tmap[:, 0, :], float(TPE), 1.0, ALU.mult, ALU.add))
            link(V.tensor_tensor(cmp_[:, :, :], tmap[:, 2, :].unsqueeze(2).to_broadcast([P, 2, NE]),
                                 const("base1").unsqueeze(1).to_broadcast([P, 2, NE]), ALU.is_equal))
            link(V.tensor_tensor(cmpc[:, :, :], cmp_[:, :, :], n3, ALU.mult))
            link(V.reduce_sum(tmap[:, 3, :], cmpc[:, :, :], AX.X))
            link(V.tensor_tensor(tmap[:, 4, :], const("tile"), tmap[:, 1, :], ALU.subtract))
            link(V.tensor_scalar(tmap[:, 4, :], tmap[:, 4, :], float(P), None, ALU.mult))
            link(V.tensor_scalar(tmap[:, 5, :], tmap[:, 3, :], -float(P), 0.0, ALU.add, ALU.max))
            link(V.tensor_tensor(tmap[:, 5, :], tmap[:, 5, :], tmap[:, 4, :], ALU.min))
            link(V.tensor_tensor(tmap[:, 6, :], tmap[:, 4, :], tmap[:, 5, :], ALU.subtract))
            link(V.tensor_scalar(tmap[:, 7, :], tmap[:, 0, :], float(TPE), None, ALU.mult))
            link(V.tensor_tensor(tmap[:, 8, :], tmap[:, 7, :], tmap[:, 5, :], ALU.add))
            link(V.tensor_scalar(tmap[:, 8, :], tmap[:, 8, :], float(SPARE), None, ALU.min))
            link(V.tensor_scalar(tmap[:, 9, :], tmap[:, 0, :], float(NE - 1), None, ALU.min))
            for c in range(2):
                for m, r in enumerate((9, 8, 6)):
                    last = V.tensor_scalar(diag[:, c, m, :], const("ident"), tmap[:, r, c:c + 1], None, ALU.mult)
                last.then_inc(S["tab_diag"], 1)
            for c in range(2):
                dve.wait_ge(S["map_mm"], c + 3)
                V.tensor_copy(tabf[:, :, c, :], (pM, pQ)[c][:, 0:3 * P].rearrange("p (m a) -> p m a", m=3)).then_inc(S["tab_ev"], 1)
            dve.wait_ge(S["tab_ev"], 2)
            tabr = tabf[0:1, :, :, :].rearrange("p m a c -> p m (a c)")
            V.memset(tabi[0:1, 0, 0:2], 0)
            V.tensor_copy(tabi[0:1, 0, 2:NT + 2], tabr[:, 0, 0:NT])
            V.tensor_copy(tabi[0:1, 1, 0:NT], tabr[:, 1, 0:NT]).then_inc(S["tab_all"], 1)
            dumpc = const("dump").unsqueeze(2).to_broadcast([P, 2, P])
            link(V.tensor_tensor(valid[:, :, :], const("tok").unsqueeze(2).to_broadcast([P, 2, P]), tabf[:, 2, :, :], ALU.is_ge))
            link(V.tensor_tensor(dumpt[:, :, :], valid[:, :, :], dumpc, ALU.mult))
            link(V.tensor_tensor(dumpt[:, :, :], dumpc, dumpt[:, :, :], ALU.subtract))
            V.sem_inc(S["tab_all"], 1)

            validr = valid[:, :, :].rearrange("p a c -> p (a c)")
            dumpr = dumpt[:, :, :].rearrange("p a c -> p (a c)")

            held = {}

            def slot(n, j):
                if cur := tile_at(n, j, 0):
                    d, jj = cur
                    if j == 0:
                        held["expert"] = entries(dve, 0, n * NCH + 2, 2 * NCH, NE - 1)
                    dve.wait_ge(S["silu_set"][jj], tile_done(n, d))
                    if not isinstance(n, int) or n + d:
                        dve.wait_ge(S["yt_set"][jj], tile_done(n, d - 1))
                    V.tensor_copy(idf[:, jj:jj + 1], xt[:, j, IDC:IDC + 1])
                    V.scalar_tensor_tensor(hid[:, jj % 2], act_[:, jj % 2], xt[:, j, bass.ds(held["expert"][j] + D, 1)],
                                           (pE, pS)[jj % 2][:, FF:2 * FF], ALU.mult, ALU.mult).then_inc(S["hid_set"][jj], 1)
                if cur := tile_at(n, j, 2):
                    d, jj = cur
                    need(dve, added[jj], at(n, d) * 16)
                    i = bass.ds(n * NCH + (j - 2), 1)
                    V.tensor_scalar(idt[:, jj:jj + 1], idf[:, jj:jj + 1], validr[:, i], dumpr[:, i], ALU.mult, ALU.add)
                    dve.wait_ge(S["dn_mm"][jj], tile_done(n, d))
                    V.tensor_copy(yt[:, jj, :], (pY, pM)[jj % 2][:, 0:D]).then_inc(S["yt_set"][jj], 1)

            slots_of(dve, slot)
            for h, (b0, b1) in enumerate(SUMS):
                dve.wait_ge(acc_ld[h], NCH * 16)
                for j in range(NCH):
                    xh = xall[:, b0:b1, :]
                    V.tensor_tensor(xh, xh, accb[:, j, b0:b1, :], ALU.add).then_inc(S["fin_set"], 1)
                    dve.wait_ge(S["fin_set"], h * NCH + j + 1)

        @block.tensor
        def _(pe):
            T = nc.tensor
            ident = const("ident")
            pe.wait_ge(S["ld_w1"], 4 * 16)
            for h in range(NG):
                for a in range(GH):
                    last = T.matmul((pQ, pT, pE, pS)[h][0:QC, a * LAT:a * LAT + LAT], wuqT[:, h * GH + a, :], wukT[:, h * GH + a, :],
                                    start=True, stop=True)
                last.then_inc(S["fold_mm"], 1)
            for k in range(DK):
                last = T.matmul(pM[:, k * ROT:k * ROT + ROT], wkvcT[:, k * P:k * P + P], wkr, start=True, stop=True)
            last.then_inc(S["fold_mm"], 1)
            pe.wait_ge(S["fold_ev"], NG + 1)
            pe.wait_ge(S["ld_w2"], 4 * 16)
            pe.wait_ge(S["ld_const"], 16)
            pe.wait_ge(S["casts"], NCASTS)

            def step(b, g):
                if cur := group(b, g, 3):
                    d, gg = cur
                    pe.wait_ge(S["eT_ev"][gg], after(b, d))
                    pe.wait_ge(S["kval_set"], after(b, d))
                    for a in range(2):
                        last = T.matmul(z2[a * LAT:a * LAT + LAT, :, :], kval, eT[:, gg % 2, a::2, :], start=True, stop=True)
                    last.then_inc(S["z_mm"][gg], 1)
                if cur := group(b, g, 0):
                    d, gg = cur
                    pe.wait_ge(S["qc_ev"], after(b, d))
                    T.matmul(pQ[:, :], qcT, wq[:, gg * GH:gg * GH + GH, :].rearrange("p h c -> p (h c)"),
                             start=True, stop=True).then_inc(S["q_mm"][gg], 1)
                if g == 2 and live(b, -2):
                    pe.wait_ge(S["sel_set"], after(b, -2))
                    T.matmul(ranks, trib[:, :], chosen[:, :], start=True, stop=False)
                    T.matmul(ranks, onesb[:, :], before[:, :], start=False, stop=True).then_inc(S["rank_mm"], 1)
                if cur := group(b, g, 1):
                    d, gg = cur
                    pe.wait_ge(S["qT_ev"][gg], after(b, d))
                    pe.wait_ge(S["kT_ev"], after(b, d))
                    pe.wait_ge(S["bias_set"], after(b, d))
                    T.matmul(pS[:, :], identb[:, :], bias[:, :].unsqueeze(1).to_broadcast([P, GH, P]), start=True, stop=True)
                    for a in range(GH):
                        last = T.matmul(s4[:, a, :], qT[:, gg % 2, a, :], kT, start=False, stop=True, skip_group_check=True)
                    last.then_inc(S["s_mm"][gg], 1)
                if isinstance(b, int) and g in foldings(b, g):
                    n = foldings(b, g)[g]
                    if n == 0:
                        pe.wait_ge(S["ld_w3"], 2 * 16)
                    else:
                        pe.wait_ge(S["fold2_ev"], n)
                    for m in range(2):
                        for a in range(2):
                            last = T.matmul(pY[a * LAT:a * LAT + LAT, m * D:m * D + D], wuvT[:, 4 * n + 2 * m + a, :],
                                            wo[:, 4 * n + 2 * m + a, :], start=True, stop=True)
                    last.then_inc(S["fold2_mm"], 1)
                if g == 0 and live(b, 0):
                    pe.wait_ge(S["ktok_set"], after(b, 0))
                    T.transpose(m4[:, 0, :], ktok, ident).then_inc(S["kT_mm"], 1)
                if cur := group(b, g, 2):
                    d, gg = cur
                    pe.wait_ge(S["norm_set"][gg], after(b, d))
                    for a in range(GH):
                        last = T.transpose(e4[:, a, :], ex[:, gg % 2, a, :], ident)
                    last.then_inc(S["eT_mm"][gg], 1)
                if g == 0 and live(b, -2):
                    pe.wait_ge(S["xrow_set"], after(b, -2))
                    for k in range(DK):
                        last = T.transpose(rowT[:, k, :], xrow[:, k * P:k * P + P], ident)
                    last.then_inc(S["x2T_mm"], 1)
                if g == 1 and live(b, -2):
                    pe.wait_ge(S["x2T_ev"], after(b, -2))
                    for k in range(DK):
                        last = T.matmul(logits, x2T[:, k, :], wrt[:, k, :], start=(k == 0), stop=(k == DK - 1))
                    last.then_inc(S["lg_mm"], 1)
                if g == 3 and live(b, 1):
                    pe.wait_ge(S["inT_ev"], after(b, 1))
                    for k in range(DK):
                        T.matmul(m4[0:QC, 0, :], wdq[:, k, :], xcT[:, k, :], start=(k == 0), stop=(k == DK - 1))
                    for k in range(DK):
                        last = T.matmul(m4[:, 1, :], xcT[:, 2 + k, :], wk[:, k, :], start=(k == 0), stop=(k == DK - 1))
                    last.then_inc(S["qk_mm"], 1)
                if cur := group(b, g, 3):
                    d, gg = cur
                    pe.wait_ge(S["zT_ev"][gg], after(b, d))
                    if gg == 0:
                        need(pe, S["x2_set"], at(b, d))
                    if isinstance(b, int) and b == 0 and gg == 0:
                        pe.wait_ge(S["fold2_ev"], FOLDS)
                    for k in range(2):
                        last = T.matmul(pY[:, 0:D], zT[:, gg % 2, k, :], wc[:, gg * 2 + k, :],
                                        start=(gg == 0 and k == 0), stop=(gg == NG - 1 and k == 1))
                    if gg == NG - 1:
                        last.then_inc(S["y_mm"], 1)
                if cur := group(b, g, 0):
                    d, gg = cur
                    pe.wait_ge(S["q_lat"][gg], after(b, d))
                    pe.wait_ge(S["rope_set"][gg], after(b, d))
                    for a in range(GH):
                        last = T.transpose(t4[:, a, :], qs[:, gg % 2, a, :], ident)
                    last.then_inc(S["qT_mm"][gg], 1)
                if g == 2 and live(b, 1):
                    pe.wait_ge(S["xn_set"], after(b, 1))
                    pe.wait_ge(S["ld_ctx"], after(b, 1) * 16)
                    need(pe, S["kT_ev"], at(b, 1))
                    for k in range(DK):
                        T.transpose(m4[:, k, :], xn[:, k * P:k * P + P], ident)
                    for k in range(DK):
                        last = T.transpose(m4[:, 2 + k, :], ctxb[:, k * P:k * P + P], ident)
                    last.then_inc(S["inT_mm"], 1)

            schedule(pe, step)

            pe.wait_ge(S["before_set"], NB + 1)
            pe.wait_ge(S["place_set"], NB)
            T.matmul(pM[0:NE, 0:1], before[:, :], onesb[:, 0:1], start=True, stop=True)
            T.matmul(pM[:, 128:128 + NE], onesb[:, :], before[:, :], start=True, stop=True).then_inc(S["map_mm"], 1)
            pe.wait_ge(S["map_s"], 4)
            T.matmul(pM[:, 256:256 + NE], ntileb[:, :], uptob[0:NE, :], start=True, stop=True).then_inc(S["map_mm"], 1)
            pe.wait_ge(S["map_s"], 5)
            for c in range(2):
                pe.wait_ge(S["tab_diag"], c + 1)
                T.matmul((pM, pQ)[c][:, 0:3 * P], onesf[:, :], diag[:, c].rearrange("p m a -> p (m a)"),
                         start=True, stop=True).then_inc(S["map_mm"], 1)
            pe.wait_ge(S["tab_ev"], 2)
            pe.wait_ge(S["tab_all"], 2)
            pe.wait_ge(S["ld_gu"], NE // 4 * 16)
            pe.wait_ge(S["ld_down"], (NG + 1 + 8 + 1) * 16)

            held = {}

            def slot(n, j):
                if j == 0:
                    held["expert"] = entries(pe, 0, n * NCH, 2 * NCH + 2, NE - 1)
                if cur := tile_at(n, j, -1):
                    d, jj = cur
                    x = (j + 1) % (2 * NCH)
                    pe.wait_ge(xt_ld[x], n * (16 // 2) + 16 * (1 + (j + 1) // (2 * NCH)))
                    for k in range(DK):
                        last = T.transpose((pQ, pT)[jj % 2][:, k * P:k * P + P], xt[:, x, k * P:k * P + P], ident)
                    last.then_inc(S["xtT_mm"][jj], 1)
                if cur := tile_at(n, j, 0):
                    d, jj = cur
                    e = held["expert"][j + 2]
                    pe.wait_ge(S["xtT_ev"][jj], tile_done(n, d))
                    for k in range(DK):
                        last = T.matmul((pE, pS)[jj % 2][:, 0:2 * FF], xtT[:, jj % 2, k, :],
                                        wgu[:, bass.ds(e, 1), k, :].rearrange("p e f -> p (e f)"), start=(k == 0), stop=(k == DK - 1))
                    last.then_inc(S["gu_mm"][jj], 1)
                if cur := tile_at(n, j, 1):
                    d, jj = cur
                    pe.wait_ge(S["hid_set"][jj], tile_done(n, d))
                    T.transpose((pZ, pR)[jj % 2][0:FF, 0:P], hid[:, jj % 2], ident).then_inc(S["hT_mm"][jj], 1)
                if cur := tile_at(n, j, 2):
                    d, jj = cur
                    e = held["expert"][j]
                    pe.wait_ge(S["hT_ev"][jj], tile_done(n, d))
                    if isinstance(n, int) and n + d == NR - 1 and jj == NCH - 1:
                        pe.wait_ge(S["yt_set"][jj - 2], tile_done(n, d))
                    T.matmul((pY, pM)[jj % 2][:, 0:D], hidT[:, jj % 2], wdn[0:FF, bass.ds(e, 1), :].rearrange("p e d -> p (e d)"),
                             start=True, stop=True).then_inc(S["dn_mm"][jj], 1)

            slots_of(pe, slot)


def table():
    import numpy as np
    c = np.zeros((P, NCONST), np.float32)
    p = np.arange(P)
    half = np.arange(HALF, dtype=np.float32) / HALF
    angle = p[:, None].astype(np.float32) * (1.0 / np.float32(10000.0) ** half).astype(np.float32)
    cos, sin = np.cos(angle), np.sin(angle)
    e = np.arange(NE)
    parts = {"ident": np.eye(P), "tri": p[:, None] < p[None, :], "cos": np.concatenate([cos, cos], 1),
             "sin": np.concatenate([-sin, sin], 1), "kidx": np.tile(p, (P, 1)), "base1": np.tile(e * TPE + 1, (P, 1)),
             "upto": p[:, None] <= e[None, :], "tile": np.stack([p, p + P], 1), "dump": NTOK + p[:, None], "tok": p[:, None],
             "thr": np.tile(np.arange(16) * P, (P, 1))}
    for n, v in parts.items():
        c[:, COL[n][0]:COL[n][1]] = v
    return c


def kernel(**inputs):
    import numpy as np
    import concourse.bacc as bacc
    from concourse.bass_utils import run_bass_kernel_spmd as run

    def w(name):
        return np.ascontiguousarray(inputs[name])

    pre, ffn = "L0_xattn_W_", "L0_ffn_W_"
    arrays = {
        "x": w("x"),
        "ctx": w("ctx_2048"),
        "seg": w("itok_BxS_0_1023").T,
        "consts": table(),
        "w_kvc": w(pre + "kvc").reshape(DK, P, LAT).transpose(1, 0, 2),
        "w_kvc_t": w(pre + "kvc").T,
        "w_dq": w(pre + "dq").reshape(DK, P, QC).transpose(1, 0, 2),
        "w_uq_t": w(pre + "uq").reshape(QC, NH, HD).transpose(2, 1, 0),
        "w_qr": w(pre + "qr").reshape(QC, NH, ROT),
        "w_uk_t": w(pre + "uk").reshape(LAT, NH, HD).transpose(2, 1, 0),
        "w_kr": w(pre + "kr"),
        "w_uv_t": w(pre + "uv").reshape(LAT, NH, HD).transpose(2, 1, 0),
        "w_o": w(pre + "o").reshape(NH, HD, D).transpose(1, 0, 2),
        "w_router": w(ffn + "router").reshape(DK, P, NE).transpose(1, 0, 2),
        "w_gu": np.concatenate([w(ffn + "gate"), w(ffn + "up")], axis=2).reshape(NE, DK, P, 2 * FF).transpose(2, 0, 1, 3),
        "w_down": w(ffn + "down").transpose(1, 0, 2),
    }
    nc = bacc.Bacc("TRN2", target_bir_lowering=False, num_devices=1)
    given, args = {}, []
    for name, a in arrays.items():
        a = np.ascontiguousarray(a)
        given["in_" + name] = a
        args.append(nc.dram_tensor("in_" + name, a.shape, mybir.dt.from_np(a.dtype), kind="ExternalInput").ap())
    args.append(nc.dram_tensor("out_0", (NB, P, D), F32, kind="ExternalOutput").ap())
    build(nc, *args)
    r = run(nc, [given], core_ids=[0])
    return r.results[0]["out_0"]
```

```python
import concourse.bass as bass
from concourse import mybir
from contextlib import ExitStack

F32 = mybir.dt.float32
BF16 = mybir.dt.bfloat16
I32 = mybir.dt.int32
ALU = mybir.AluOpType
ACT = mybir.ActivationFunctionType
AX = mybir.AxisListType

P = 128
NB = 16
D = 256
DK = D // P
NH, LAT, ROT = 16, 64, 64
QC = 96
HD = 128
HALF = ROT // 2
GH = 4
NG = NH // GH
NE, FF, TOPK = 64, 96, 8
NTOK = NB * P
EPS = 1e-5
NEG = -1e30
LOOKBACK = 8
SCALE = float((HD + ROT) ** -0.5)
TPE = NTOK
ROW = D + NE + 4
IDC = D + NE
NCH = 4
XB = 6
ACCS = 3
UNROLL = 12
NT = -(-((NTOK * TOPK - NE) // P + NE) // UNROLL) * UNROLL
NCASTS = 5
STATS = [(0, 1), (1, 4), (4, 8), (8, 12), (12, NB)]
SUMS = [(0, 1), (1, 3), (3, 5), (5, 8), (8, 11), (11, 13), (13, 15), (15, 16)]
FOLDS = 4
ZEROS = ACCS * (NB + 1)
SPARE = NE * TPE

CONSTS = [("ident", P), ("tri", P), ("cos", ROT), ("sin", ROT), ("kidx", P), ("base1", NE),
          ("upto", NE), ("tile", 2), ("dump", 1), ("tok", 1), ("thr", 16)]
COL = {}
NCONST = 0
for _n, _w in CONSTS:
    COL[_n] = (NCONST, NCONST + _w)
    NCONST += _w


def build(nc, x, ctx, seg, consts, w_kvc, w_kvc_t, w_dq, w_uq_t, w_qr, w_uk_t, w_kr, w_uv_t, w_o,
          w_router, w_gu, w_down, out):
    rows = nc.dram_tensor("rows", (NE * TPE + P, ROW), F32)
    accs = [nc.dram_tensor(f"acc{j}", (NTOK + P, D), F32) for j in range(ACCS)]
    es = ExitStack()
    with es:
        def sb(name, shape, dt=F32):
            return es.enter_context(nc.sbuf_tensor(name, shape, dt))

        def pb(name):
            return es.enter_context(nc.psum_tensor(name, [P, 512], F32))

        def sem(name):
            return es.enter_context(nc.semaphore(name))

        wgu = sb("wgu", [P, NE, DK, 2 * FF])
        wdn = sb("wdn", [P, NE, D])
        xall = sb("xall", [P, NB, D])
        cst = sb("cst", [P, NCONST])

        def const(name):
            return cst[:, COL[name][0]:COL[name][1]]

        arena = wdn[:, :, :].rearrange("p e d -> p (e d)")
        used = [0]

        def carve(n):
            used[0] += n
            assert used[0] <= NE * D
            return arena[:, NE * D - used[0]:NE * D - used[0] + n]

        srow = carve(2 * ROW).rearrange("p (a r) -> p a r", a=2)
        DOWN_LAST = (NE * D - used[0]) // D
        wc = carve(NH // 2 * D).rearrange("p (n d) -> p n d", d=D)
        wdq = carve(DK * QC).rearrange("p (k c) -> p k c", k=DK)
        wk = carve(DK * P).rearrange("p (k c) -> p k c", k=DK)
        xn = carve(D)
        ctxb = carve(D)
        xcT = carve(4 * P).rearrange("p (k c) -> p k c", k=4)
        qcT = carve(P)[0:QC, :]
        ktok = carve(P)
        kT = carve(P)
        kval = carve(LAT)
        ropet = carve(2 * GH * ROT).rearrange("p (a h c) -> p a h c", a=2, h=GH)
        kropet = carve(ROT)
        qs = carve(2 * GH * P).rearrange("p (a h c) -> p a h c", a=2, h=GH)
        qT = carve(2 * GH * P).rearrange("p (a h c) -> p a h c", a=2, h=GH)
        ex = carve(2 * GH * P).rearrange("p (a h c) -> p a h c", a=2, h=GH)
        eT = carve(2 * GH * P).rearrange("p (a h c) -> p a h c", a=2, h=GH)
        zero = carve(D)
        zT = carve(2 * GH * LAT).rearrange("p (a k c) -> p a k c", a=2, k=2)
        smin = carve(2 * GH).rearrange("p (a h) -> p a h", a=2)
        esum = carve(2 * GH).rearrange("p (a h) -> p a h", a=2)
        rsum = carve(2 * GH).rearrange("p (a h) -> p a h", a=2)
        DOWN_MID = (NE * D - used[0]) // D
        wq = carve(NH * P)[0:QC, :].rearrange("p (h c) -> p h c", h=NH)
        DOWN_FREE = (NE * D - used[0]) // D
        early = wgu[:, :, :, :].rearrange("p e k f -> p (e k f)")
        wuqT = early[:, 0:NH * QC].rearrange("p (h c) -> p h c", h=NH)
        wukT = early[:, 2048:2048 + NH * LAT].rearrange("p (h c) -> p h c", h=NH)
        wuvT = early[:, 4096:4096 + NH * LAT].rearrange("p (h c) -> p h c", h=NH)
        wo = early[:, 6144:6144 + NH * D].rearrange("p (h d) -> p h d", h=NH)
        wkvcT = early[0:LAT, 12288:12288 + D]
        wkr = early[0:LAT, 12800:12800 + ROT]

        accb = early[:, 0:NB * ACCS * D].rearrange("p (a b d) -> p a b d", a=ACCS, d=D)

        scratch = sb("scratch", [P, NCH * D])
        taken = [0]

        def short(*shape):
            n = 1
            for d in shape:
                n *= d
            taken[0] += n
            assert taken[0] <= NCH * D
            v = scratch[:, taken[0] - n:taken[0]]
            return v if len(shape) == 1 else v.rearrange("p (a b) -> p a b", a=shape[0])

        yt = scratch[:, :].rearrange("p (j d) -> p j d", j=NCH)
        diag = scratch[:, 0:6 * P].rearrange("p (c m a) -> p c m a", c=2, m=3)
        segi = sb("segi", [P, NB], I32)
        segf = sb("segf", [P, NB])
        seglo = sb("seglo", [P, NB])
        biast = short(2, P)
        bias = sb("bias", [P, P], BF16)
        identb = sb("identb", [P, P], BF16)
        trib = sb("trib", [P, P], BF16)
        uptob = sb("uptob", [P, NE], BF16)
        onesf = sb("onesf", [P, P])
        onesb = sb("onesb", [P, P], BF16)
        stats = short(NB, 6)
        mv = sb("mv", [P, NB, 2])
        rstd = sb("rstd", [P, NB])
        mhalf = sb("mhalf", [P, NB])
        stats2 = sb("stats2", [P, 6])
        mv2 = sb("mv2", [P, 2])
        rstd2 = sb("rstd2", [P, 1])
        wrt = sb("wrt", [P, DK, NE])
        xrow = sb("xrow", [P, ROW])
        x2T = short(DK, P)
        logit = short(NE)
        rest = short(NE)
        top = sb("top", [P, TOPK])
        ntop = sb("ntop", [P, 1])
        prob = short(NE)
        psel = short(NE)
        psum_ = sb("psum_", [P, 1])
        pinv = sb("pinv", [P, 1])
        chosen = sb("chosen", [P, NE], BF16)
        before = sb("before", [P, NE], BF16)
        place = short(NE)
        placem = short(NE)
        slot8 = sb("slot8", [P, TOPK])
        slots = sb("slots", [P, 2, TOPK], I32)
        cnt = sb("cnt", [NE, 16])
        ntile = sb("ntile", [NE, 1])
        ntileb = sb("ntileb", [NE, P], BF16)
        cmp_ = sb("cmp_", [P, 2, NE])
        cmpc = sb("cmpc", [P, 2, NE])
        cum = sb("cum", [P, 3, NE])
        tmap = sb("tmap", [P, 10, 2])
        tabi = sb("tabi", [1, 2, NT + 2], I32)
        valid = sb("valid", [P, 2, P])
        dumpt = sb("dumpt", [P, 2, P])
        xt = sb("xt", [P, XB, ROW])
        tabf = xt[:, :, :].rearrange("p j r -> p (j r)")[:, 0:6 * P].rearrange("p (m c a) -> p m c a", m=3, c=2)
        xtT = sb("xtT", [P, 2, DK, P])
        act_ = sb("act_", [P, 2, FF])
        hid = sb("hid", [P, 2, FF])
        hidT = sb("hidT", [FF, 2, P])
        idf = sb("idf", [P, NCH])
        idt = sb("idt", [P, NCH], I32)

        pQ, pT, pE, pS, pZ, pR, pY, pM = (pb(n) for n in ("pQ", "pT", "pE", "pS", "pZ", "pR", "pY", "pM"))
        q4 = pQ[:, :].rearrange("p (h c) -> p h c", h=GH)
        t4 = pT[:, :].rearrange("p (h c) -> p h c", h=GH)
        e4 = pE[:, :].rearrange("p (h c) -> p h c", h=GH)
        s4 = pS[:, :].rearrange("p (h c) -> p h c", h=GH)
        z2 = pZ[:, 0:2 * P].rearrange("p (k c) -> p k c", k=2)
        m4 = pM[:, :].rearrange("p (k c) -> p k c", k=4)
        rowT = pR[:, 0:2 * P].rearrange("p (k c) -> p k c", k=2)
        logits = pR[:, 256:256 + NE]
        ranks = pR[:, 384:384 + NE]

        S = {}

        def s_(name):
            if name not in S:
                S[name] = sem(name)
            return S[name]

        for n in ("ld_const ld_x0 ld_x1 ld_x ld_seg ld_w1 ld_w2 ld_w3 ld_ctx ld_gu ld_down "
                  "casts mhalf_set rowid_set fold_mm fold_ev fold2_mm fold2_ev prefilled zeroed fillrow_set "
                  "segf_set mv_set var_set rstd_set xn_set "
                  "inT_mm inT_ev qk_mm qc_ev k_ev krope_b ktok_set kT_mm kT_ev kval_set "
                  "bias_b bias_set "
                  "y_mm x2_set st2 mv2_set var2 rstd2_set xrow_set x2T_mm x2T_ev lg_mm lg_ev top_set rest_set ntop_set "
                  "prob_set sel_set psel_set pinv_set rank_mm place_set placem_set slot8_set slots_set "
                  "before_set srow_set sent ids_next "
                  "map_mm map_s tab_diag tab_ev tab_all "
                  "passed_pool passed_dve stored fin_set").split():
            s_(n)
        for n in ("q_mm q_lat ropeb rope_set qT_mm qT_ev s_mm min_set exp_set rs_set norm_set eT_mm eT_ev z_mm zT_ev").split():
            S[n] = [sem(f"{n}{i}") for i in range(NG)]
        for tile_stage, group_stage in (("xtT_mm", "qT_mm"), ("xtT_ev", "qT_ev"), ("gu_mm", "s_mm"), ("silu_set", "exp_set"),
                                        ("hid_set", "norm_set"), ("hT_mm", "eT_mm"), ("hT_ev", "eT_ev"), ("dn_mm", "z_mm"),
                                        ("yt_set", "min_set")):
            S[tile_stage] = S[group_stage]
        xt_ld = [sem(f"xt_ld{j}") for j in range(XB)]
        added = [sem(f"added{j}") for j in range(ACCS)]
        acc_ld = [sem(f"acc_ld{j}") for j in range(len(SUMS))]

        block = es.enter_context(nc.Block())

        def group(b, g, lag):
            d, gg = (g - lag) // NG, (g - lag) % NG
            return (d, gg) if live(b, d) else None

        def live(b, d):
            return not isinstance(b, int) or 0 <= b + d < NB

        def at(b, d):
            return b + d if d else b

        def folds(b, g):
            return isinstance(b, int) and b == 0 and g < FOLDS

        def own(b, d):
            return int(isinstance(b, int) and b + d == NB - 1)

        def after(b, d):
            return at(b, d + 1)

        def need(eng, s, count):
            if isinstance(count, int) and count <= 0:
                return
            eng.wait_ge(s, count)

        def passed(eng):
            eng.sem_inc(S["passed_pool" if eng is nc.gpsimd else "passed_dve"], 1)

        def schedule(eng, step):
            for b, g in [(-1, 2), (-1, 3)] + [(b, g) for b in (0, 1, 2) for g in range(NG)]:
                step(b, g)
            with eng.Fori(3, NB - 1) as b:
                for g in range(NG):
                    step(b, g)
            for b, g in [(b, g) for b in range(NB - 1, NB + 2) for g in range(NG)]:
                step(b, g)

        def tile_at(n, j, lag):
            return None if isinstance(n, int) and not 0 <= n * UNROLL + j - lag < NT else j - lag

        def early_tile(n, t):
            return isinstance(n, int) and n * UNROLL + t < 0

        def tile_done(n, t):
            return n * (UNROLL // NCH) + (t // NCH + 1 + NB)

        def rows_loaded(n, t):
            return n * (16 * UNROLL // XB) + 16 * (t // XB + 1)

        def addition_done(n, t):
            return n * (16 * UNROLL // ACCS) + 16 * (t // ACCS + 1)

        def entries(eng, row, first, count, top_value):
            _, got = nc.values_load_multi_w_load_instructions(
                tabi[0:1, row, bass.ds(first, count)], engines=(eng.engine,), min_val=0, max_val=top_value,
                skip_runtime_bounds_check_because="the table's makers clamp them")
            return got

        def slots_of(eng, slot):
            slot(-1, UNROLL - 1)
            for j in range(UNROLL):
                slot(0, j)
            with eng.Fori(1, NT // UNROLL - 1) as n:
                for j in range(UNROLL):
                    slot(n, j)
            for j in range(UNROLL + 2):
                slot(NT // UNROLL - 1, j)

        @block.sync
        def _(sp):
            sp.dma_start(cst[:, :], consts).then_inc(S["ld_const"], 16)
            sp.dma_start(segi[:, :], seg).then_inc(S["ld_seg"], 16)
            sp.dma_start(xall[:, 0, :], x[0]).then_inc(S["ld_x0"], 16)
            sp.dma_start(ctxb, ctx[0]).then_inc(S["ld_ctx"], 16)
            for dst, src in ((wukT, w_uk_t), (wuqT, w_uq_t), (wkvcT, w_kvc_t), (wkr, w_kr)):
                sp.dma_start(dst, src).then_inc(S["ld_w1"], 16)
            for dst, src in ((wdq, w_dq), (wk[:, :, 0:LAT], w_kvc), (wq[:, :, LAT:P], w_qr), (wrt[:, :, :], w_router)):
                sp.dma_start(dst, src).then_inc(S["ld_w2"], 16)

            def load_down(e0, e1):
                sp.dma_start(wdn[0:FF, e0:e1, :], w_down[:, e0:e1, :]).then_inc(S["ld_down"], 16)

            def step(b, g):
                first = isinstance(b, int) and b == -1 and g == 2
                if g == 1 and live(b, 1):
                    need(sp, S["inT_mm"], at(b, 1))
                    sp.dma_start(ctxb, ctx[bass.ds(at(b, 1), 1), :, :].rearrange("b t d -> (b t) d")).then_inc(S["ld_ctx"], 16)
                if first:
                    soon = STATS[1][1]
                    sp.dma_start(xall[:, 1:soon, :], x[1:soon].rearrange("b t d -> t b d")).then_inc(S["ld_x1"], 16)
                    for dst, src in ((wuvT, w_uv_t), (wo, w_o)):
                        sp.dma_start(dst, src).then_inc(S["ld_w3"], 16)
                    sp.dma_start(xall[:, soon:NB, :], x[soon:NB].rearrange("b t d -> t b d")).then_inc(S["ld_x"], 16)
                if live(b, 0):
                    sp.wait_ge(S["q_mm"][g], after(b, 0))
                    if isinstance(b, int) and b < 2:
                        if b == 0 and g == 0:
                            sp.wait_ge(S["fillrow_set"], 4)
                            sp.dma_start(rows.ap()[SPARE:SPARE + P, :], srow[:, 0, :]).then_inc(S["prefilled"], 16)
                        e0 = (b * NG + g) * (NE // 8)
                        sp.dma_start(rows.ap()[e0 * TPE:(e0 + NE // 8) * TPE, :].rearrange("(e t) r -> t e r", t=TPE)[0:P],
                                     srow[:, 0, :].unsqueeze(1).to_broadcast([P, NE // 8, ROW])).then_inc(S["prefilled"], 16)
                    if g < ACCS:
                        sp.dma_start(accs[g].ap()[bass.ds(b * P, P), :], zero).then_inc(S["zeroed"], 16)
                        if isinstance(b, int) and b == NB - 1:
                            sp.dma_start(accs[g].ap()[NTOK:NTOK + P, :], zero).then_inc(S["zeroed"], 16)
                if isinstance(b, int) and b == 2:
                    load_down(DOWN_FREE * g // NG, DOWN_FREE * (g + 1) // NG)
                if isinstance(b, int) and b == NB and g == 0:
                    sp.wait_ge(S["q_mm"][NG - 1], NB)
                    load_down(DOWN_FREE, DOWN_MID)
                if g == 3 and live(b, 0):
                    if isinstance(b, int) and b == 0:
                        sp.wait_ge(S["fold_mm"], NG + 1)
                        sp.wait_ge(S["fold2_mm"], FOLDS)
                    sp.dma_start(wgu[:, bass.ds(b * 4, 4), :, :], w_gu[:, bass.ds(b * 4, 4), :, :]).then_inc(S["ld_gu"], 16)

            schedule(sp, step)
            sp.wait_ge(S["zeroed"], ZEROS * 16)
            paces = [("x2_set", NB), ("xrow_set", NB), ("lg_mm", NB), ("sel_set", NB), ("slots_set", NB),
                     ("map_mm", 1), ("map_mm", 2), ("tab_diag", 1)]
            for k, (name, count) in enumerate(paces):
                sp.wait_ge(S[name], count)
                load_down(DOWN_MID + (DOWN_LAST - DOWN_MID) * k // len(paces), DOWN_MID + (DOWN_LAST - DOWN_MID) * (k + 1) // len(paces))

            sp.wait_ge(S["tab_all"], 2)

            def load_tiles(n):
                first = entries(sp, 1, n * UNROLL, UNROLL, SPARE)
                if isinstance(n, int):
                    sp.wait_ge(S["sent"], NB * TOPK * 16)
                for t in range(UNROLL):
                    if not early_tile(n, t - XB):
                        sp.wait_ge(S["hid_set"][(t - XB) % NCH], tile_done(n, t - XB))
                    sp.dma_start(xt[:, t % XB, :], rows.ap()[bass.ds(first[t], P), :]).then_inc(xt_ld[t % XB], 16)
                    if isinstance(n, int) and t == XB - 1:
                        load_down(DOWN_LAST, NE)

            load_tiles(0)
            with sp.Fori(1, NT // UNROLL) as n:
                load_tiles(n)

            for j in range(ACCS):
                sp.wait_ge(added[j], NT // ACCS * 16)
            sp.wait_ge(S["gu_mm"][NCH - 1], tile_done(0, NT - 1))
            for h, (b0, b1) in enumerate(SUMS):
                for j in range(ACCS):
                    sp.dma_start(accb[:, j, b0:b1, :],
                                 accs[j].ap()[b0 * P:b1 * P, :].rearrange("(b t) d -> t b d", t=P)).then_inc(acc_ld[h], 16)
            for h, (b0, b1) in enumerate(SUMS):
                sp.wait_ge(S["fin_set"], ACCS * (h + 1))
                sp.dma_start(out[b0:b1].rearrange("b t d -> t b d"), xall[:, b0:b1, :]).then_inc(S["stored"], 16)
            sp.wait_ge(S["stored"], len(SUMS) * 16)

        @block.gpsimd
        def _(pool):
            nc.gpsimd.memset(onesb[:, :], 1.0).then_inc(S["casts"], 1)
            nc.gpsimd.memset(onesf[:, :], 1.0).then_inc(S["casts"], 1)
            nc.gpsimd.memset(before[:, :], 0.0).then_inc(S["before_set"], 1)
            nc.gpsimd.memset(mhalf[:, :], -0.5).then_inc(S["mhalf_set"], 1)
            nc.gpsimd.memset(srow[:, 0, :], 0.0).then_inc(S["fillrow_set"], 1)
            nc.gpsimd.memset(zero, 0.0).then_inc(S["fillrow_set"], 1)
            nc.gpsimd.memset(xrow[:, IDC:ROW], 0.0).then_inc(S["rowid_set"], 1)
            pool.wait_ge(S["ld_const"], 16)
            nc.gpsimd.tensor_copy(identb[:, :], const("ident")).then_inc(S["casts"], 1)
            nc.gpsimd.tensor_copy(trib[:, :], const("tri")).then_inc(S["casts"], 1)
            nc.gpsimd.tensor_copy(uptob[:, :], const("upto")).then_inc(S["casts"], 1)
            pool.wait_ge(S["fillrow_set"], 2)
            nc.gpsimd.tensor_copy(srow[:, 0, IDC:IDC + 1], const("dump")).then_inc(S["fillrow_set"], 1)
            pool.wait_ge(S["rowid_set"], 1)
            nc.gpsimd.tensor_scalar(xrow[:, IDC:IDC + 1], const("tok"), -float(P), None, ALU.add).then_inc(S["fillrow_set"], 1)
            def rsqrt(n):
                first, end = STATS[n]
                pool.wait_ge(S["var_set"], n + 1)
                nc.gpsimd.tensor_tensor(rstd[:, first:end], mv[:, first:end, 1], mhalf[:, first:end], ALU.pow).then_inc(S["rstd_set"], 1)

            rsqrt(0)

            EARLY = 1

            def send(b, d, choices):
                a = own(b, d)
                if choices[0] == 0:
                    pool.wait_ge(S["srow_set"], after(b, d))
                    pool.wait_ge(S["slots_set"], after(b, d))
                    passed(pool)
                for k in choices:
                    nc.gpsimd.indirect_dma_start(rows.ap(), bass.IndirectOffsetOnAxis(ap=slots[:, a, k:k + 1], axis=0),
                                                 srow[:, a, :], None).then_inc(S["sent"], 16)

            def step(b, g):
                if cur := group(b, g, 0):
                    d, gg = cur
                    pool.wait_ge(S["ropeb"][gg], after(b, d))
                    nc.gpsimd.tensor_tensor(qs[:, gg % 2, :, LAT:P], ropet[:, 0], ropet[:, 1], ALU.add).then_inc(S["rope_set"][gg], 1)
                if isinstance(b, int) and b == 0:
                    rsqrt(g + 1)
                if isinstance(b, int) and b == NB and g == 2:
                    send(b, -2, range(EARLY))
                d = -1
                if g == 2 and live(b, d):
                    pool.wait_ge(S["var2"], after(b, d))
                    nc.gpsimd.tensor_tensor(rstd2[:, :], mv2[:, 1:2], mhalf[:, 0:1], ALU.pow).then_inc(S["rstd2_set"], 1)
                if g < 2 and live(b, -3):
                    if isinstance(b, int) and b == NB + 1:
                        if g == 0:
                            send(b, -3, range(EARLY, TOPK))
                    else:
                        send(b, -3, range(g * TOPK // 2, (g + 1) * TOPK // 2))

            schedule(pool, step)
            for g in range(2):
                step(NB + 2, g)

            def add_tile(n, t):
                p, a = t % NCH, t % ACCS
                pool.wait_ge(S["yt_set"][p], tile_done(n, t))
                if not early_tile(n, t - ACCS):
                    pool.wait_ge(added[a], addition_done(n, t - ACCS))
                passed(pool)
                nc.gpsimd.indirect_dma_start(accs[a].ap(), bass.IndirectOffsetOnAxis(ap=idt[:, p:p + 1], axis=0),
                                             yt[:, p, :], None, compute_op=ALU.add).then_inc(added[a], 16)

            pool.wait_ge(S["zeroed"], ZEROS * 16)
            for t in range(UNROLL):
                add_tile(0, t)
            with pool.Fori(1, NT // UNROLL) as n:
                for t in range(UNROLL):
                    add_tile(n, t)

        @block.scalar
        def _(act):
            act.wait_ge(S["inT_mm"], 1)
            nc.scalar.activation(xcT, m4, ACT.Copy).then_inc(S["inT_ev"], 1)
            for h in range(NG):
                act.wait_ge(S["fold_mm"], h + 1)
                nc.scalar.activation(wq[:, h * GH:h * GH + GH, 0:LAT],
                                     (pQ, pT, pE, pS)[h][0:QC, 0:GH * LAT].rearrange("p (h c) -> p h c", h=GH),
                                     ACT.Copy).then_inc(S["fold_ev"], 1)
            act.wait_ge(S["fold_mm"], NG + 1)
            nc.scalar.activation(wk[:, :, LAT:P], pY[:, 0:DK * ROT].rearrange("p (k c) -> p k c", k=DK), ACT.Copy).then_inc(S["fold_ev"], 1)

            def step(b, g):
                if folds(b, g):
                    act.wait_ge(S["fold2_mm"], g + 1)
                    n = 2 * g
                    nc.scalar.activation(wc[:, n:n + 2, :], pY[:, :].rearrange("p (n d) -> p n d", n=2), ACT.Copy).then_inc(S["fold2_ev"], 1)
                if cur := group(b, g, 3):
                    d, gg = cur
                    act.wait_ge(S["z_mm"][gg], after(b, d))
                    nc.scalar.activation(zT[:, gg % 2], z2, ACT.Copy).then_inc(S["zT_ev"][gg], 1)
                if g == 0 and live(b, 0):
                    act.wait_ge(S["kT_mm"], after(b, 0))
                    nc.scalar.activation(kT, m4[:, 0, :], ACT.Copy, scale=-SCALE).then_inc(S["kT_ev"], 1)
                if cur := group(b, g, 0):
                    d, gg = cur
                    act.wait_ge(S["ropeb"][gg], after(b, d))
                    nc.scalar.activation(qs[:, gg % 2, :, 0:LAT], q4[:, :, 0:LAT], ACT.Copy).then_inc(S["q_lat"][gg], 1)
                if g == 2 and live(b, -2):
                    act.wait_ge(S["ntop_set"], after(b, -2))
                    nc.scalar.activation(prob, logit, ACT.Exp, bias=ntop[:, :], scale=1.0).then_inc(S["prob_set"], 1)
                if cur := group(b, g, 2):
                    d, gg = cur
                    act.wait_ge(S["eT_mm"][gg], after(b, d))
                    nc.scalar.activation(eT[:, gg % 2], e4, ACT.Copy).then_inc(S["eT_ev"][gg], 1)
                if g == 3 and live(b, 1):
                    act.wait_ge(S["qk_mm"], after(b, 1))
                    nc.scalar.activation(qcT, m4[0:QC, 0, :], ACT.Copy).then_inc(S["qc_ev"], 1)
                    nc.scalar.activation(ktok[:, 0:LAT], m4[:, 1, 0:LAT], ACT.Copy).then_inc(S["k_ev"], 1)
                if cur := group(b, g, 1):
                    d, gg = cur
                    act.wait_ge(S["min_set"][gg], after(b, d))
                    for a in range(GH):
                        last = nc.scalar.activation(ex[:, gg % 2, a, :], s4[:, a, :], ACT.Exp, bias=smin[:, gg % 2, a:a + 1], scale=-1.0,
                                                    accum_out=esum[:, gg % 2, a:a + 1])
                    last.then_inc(S["exp_set"][gg], 1)
                if cur := group(b, g, 0):
                    d, gg = cur
                    act.wait_ge(S["qT_mm"][gg], after(b, d))
                    nc.scalar.activation(qT[:, gg % 2], t4, ACT.Copy).then_inc(S["qT_ev"][gg], 1)
                if g == 0 and live(b, -2):
                    act.wait_ge(S["x2T_mm"], after(b, -2))
                    nc.scalar.activation(x2T, rowT, ACT.Copy).then_inc(S["x2T_ev"], 1)
                if g == 2 and live(b, 1) and live(b, 0):
                    act.wait_ge(S["inT_mm"], after(b, 1))
                    nc.scalar.activation(xcT, m4, ACT.Copy).then_inc(S["inT_ev"], 1)

            schedule(act, step)
            def slot(n, j):
                if (t := tile_at(n, j, -1)) is not None:
                    p = t % NCH
                    act.wait_ge(S["xtT_mm"][p], tile_done(n, t))
                    nc.scalar.activation(xtT[:, p % 2], (pQ, pT)[p % 2][:, 0:D].rearrange("p (k c) -> p k c", k=DK), ACT.Copy).then_inc(S["xtT_ev"][p], 1)
                if (t := tile_at(n, j, 0)) is not None:
                    p = t % NCH
                    act.wait_ge(S["gu_mm"][p], tile_done(n, t))
                    nc.scalar.activation(act_[:, p % 2], (pE, pS)[p % 2][:, 0:FF], ACT.Silu).then_inc(S["silu_set"][p], 1)
                if (t := tile_at(n, j, 1)) is not None:
                    p = t % NCH
                    act.wait_ge(S["hT_mm"][p], tile_done(n, t))
                    nc.scalar.activation(hidT[:, p % 2], (pZ, pR)[p % 2][0:FF, 0:P], ACT.Copy).then_inc(S["hT_ev"][p], 1)

            slots_of(act, slot)

        @block.vector
        def _(dve):
            V = nc.vector
            dve.wait_ge(S["ld_seg"], 16)
            V.tensor_copy(segf[:, :], segi[:, :]).then_inc(S["segf_set"], 1)
            dve.wait_ge(S["segf_set"], 1)
            V.tensor_scalar(seglo[:, :], segf[:, :], -float(LOOKBACK), None, ALU.add).then_inc(S["segf_set"], 1)
            def norm(b):
                V.tensor_scalar(xn, xall[:, bass.ds(b, 1), :].rearrange("p b d -> p (b d)"),
                                mv[:, bass.ds(b, 1), 0], rstd[:, bass.ds(b, 1)], ALU.subtract, ALU.mult).then_inc(S["xn_set"], 1)

            def statistics(n):
                first, end = STATS[n]
                dve.wait_ge(S[("ld_x0", "ld_x1", "ld_x", "ld_x", "ld_x")[n]], 16)
                for b in range(first, end):
                    V.bn_stats(stats[:, b, :], xall[:, b, :]).then_inc(S["mv_set"], 1)
                dve.wait_ge(S["mv_set"], first + end)
                for b in range(first, end):
                    V.bn_aggr(mv[:, b, :], stats[:, b, :]).then_inc(S["mv_set"], 1)
                dve.wait_ge(S["mv_set"], 2 * end)
                V.tensor_scalar(mv[:, first:end, 1], mv[:, first:end, 1], EPS, None, ALU.add).then_inc(S["var_set"], 1)

            statistics(0)
            dve.wait_ge(S["rstd_set"], 1)
            norm(0)
            dve.wait_ge(S["segf_set"], 2)
            dve.wait_ge(S["ld_const"], 16)
            dve.wait_ge(S["fillrow_set"], 4)
            dve.wait_ge(S["casts"], NCASTS)

            def last_batches(b):
                return isinstance(b, int) and b >= NB

            def expert_weights(b):
                d = -2
                dve.wait_ge(S["prob_set"], after(b, d))
                dve.wait_ge(S["sel_set"], after(b, d))
                V.tensor_tensor_reduce(out=psel, in0=prob, in1=chosen[:, :], scale=1.0, scalar=0.0,
                                       op0=ALU.mult, op1=ALU.add, accum_out=psum_[:, :]).then_inc(S["psel_set"], 1)
                dve.wait_ge(S["psel_set"], after(b, d))
                V.reciprocal(pinv[:, :], psum_[:, :]).then_inc(S["pinv_set"], 1)
                dve.wait_ge(S["pinv_set"], after(b, d))
                V.tensor_scalar(xrow[:, D:D + NE], psel, pinv[:, :], None, ALU.mult)
                V.tensor_scalar(xrow[:, IDC:IDC + 1], xrow[:, IDC:IDC + 1], float(P), None, ALU.add).then_inc(S["ids_next"], 1)

            def send_rows(b):
                d = -2
                V.tensor_tensor(before[:, :], before[:, :], chosen[:, :], ALU.add).then_inc(S["before_set"], 1)
                dve.wait_ge(S["place_set"], after(b, d))
                V.tensor_tensor(placem, place, chosen[:, :], ALU.mult).then_inc(S["placem_set"], 1)
                dve.wait_ge(S["placem_set"], after(b, d))
                passed(dve)
                V.max(slot8[:, :], placem).then_inc(S["slot8_set"], 1)
                dve.wait_ge(S["slot8_set"], after(b, d))
                a = own(b, d)
                if a == 0:
                    need(dve, S["sent"], at(b, d) * (TOPK * 16))
                if isinstance(b, int) and b == 2:
                    dve.wait_ge(S["prefilled"], 9 * 16)
                V.tensor_scalar(slots[:, a, :], slot8[:, :], -1.0, None, ALU.add).then_inc(S["slots_set"], 1)
                dve.wait_ge(S["ids_next"], after(b, d))
                V.tensor_copy(srow[:, a, :], xrow[:, :]).then_inc(S["srow_set"], 1)

            def step(b, g):
                if cur := group(b, g, 2):
                    d, gg = cur
                    dve.wait_ge(S["exp_set"][gg], after(b, d))
                    V.reciprocal(rsum[:, gg % 2], esum[:, gg % 2]).then_inc(S["rs_set"][gg], 1)
                    dve.wait_ge(S["rs_set"][gg], after(b, d))
                    V.tensor_tensor(ex[:, gg % 2], ex[:, gg % 2], rsum[:, gg % 2].unsqueeze(2).to_broadcast([P, GH, P]),
                                    ALU.mult).then_inc(S["norm_set"][gg], 1)
                cosb = const("cos").unsqueeze(1).to_broadcast([P, GH, ROT])
                if cur := group(b, g, 0):
                    d, gg = cur
                    dve.wait_ge(S["q_mm"][gg], after(b, d))
                    V.tensor_tensor(ropet[:, 0], q4[:, :, LAT:P], cosb, ALU.mult)
                    for a in range(2):
                        last = V.tensor_tensor(
                            ropet[:, 1, :, a * HALF:a * HALF + HALF], q4[:, :, LAT + (1 - a) * HALF:LAT + (2 - a) * HALF],
                            const("sin")[:, a * HALF:a * HALF + HALF].unsqueeze(1).to_broadcast([P, GH, HALF]), ALU.mult)
                    last.then_inc(S["ropeb"][gg], 1)
                if g == 1 and live(b, 1):
                    if isinstance(b, int) and b < 2:
                        dve.wait_ge(S["rstd_set"], (2, len(STATS))[b])
                    norm(at(b, 1))
                if g == 2 and live(b, -2):
                    dve.wait_ge(S["rank_mm"], after(b, -2))
                    V.tensor_tensor(place, ranks, const("base1"), ALU.add).then_inc(S["place_set"], 1)
                if cur := group(b, g, 1):
                    d, gg = cur
                    dve.wait_ge(S["s_mm"][gg], after(b, d))
                    V.tensor_reduce(smin[:, gg % 2], s4, AX.X, ALU.min).then_inc(S["min_set"][gg], 1)
                if g == 0 and live(b, 0):
                    V.tensor_scalar(biast[:, 0, :], const("kidx"), segf[:, bass.ds(at(b, 0), 1)], -NEG, ALU.is_gt, ALU.mult)
                    V.tensor_scalar(biast[:, 1, :], const("kidx"), seglo[:, bass.ds(at(b, 0), 1)], -NEG, ALU.is_lt, ALU.mult).then_inc(S["bias_b"], 1)
                    dve.wait_ge(S["bias_b"], after(b, 0))
                    V.tensor_tensor(bias[:, :], biast[:, 0, :], biast[:, 1, :], ALU.add).then_inc(S["bias_set"], 1)
                if g == 2 and live(b, 0):
                    need(dve, S["z_mm"][NG - 1], at(b, 0))
                    dve.wait_ge(S["k_ev"], after(b, 0))
                    V.tensor_copy(kval, ktok[:, 0:LAT]).then_inc(S["kval_set"], 1)
                if g == 2 and live(b, -2) and last_batches(b):
                    expert_weights(b)
                    send_rows(b)
                d = -1
                if g == 2 and live(b, d):
                    dve.wait_ge(S["y_mm"], after(b, d))
                    xb = xall[:, bass.ds(at(b, d), 1), :].rearrange("p b d -> p (b d)")
                    V.tensor_tensor(xb, xb, pY[:, 0:D], ALU.add).then_inc(S["x2_set"], 1)
                    dve.wait_ge(S["x2_set"], after(b, d))
                    passed(dve)
                    V.bn_stats(stats2[:, :], xb).then_inc(S["st2"], 1)
                    dve.wait_ge(S["st2"], after(b, d))
                    passed(dve)
                    V.bn_aggr(mv2[:, :], stats2[:, :]).then_inc(S["mv2_set"], 1)
                    dve.wait_ge(S["mv2_set"], after(b, d))
                    V.tensor_scalar(mv2[:, 1:2], mv2[:, 1:2], EPS, None, ALU.add).then_inc(S["var2"], 1)
                d = -2
                if g == 1 and live(b, d):
                    dve.wait_ge(S["lg_mm"], after(b, d))
                    V.tensor_copy(logit, logits).then_inc(S["lg_ev"], 1)
                    dve.wait_ge(S["lg_ev"], after(b, d))
                    passed(dve)
                    V.max(top[:, :], logit).then_inc(S["top_set"], 1)
                    dve.wait_ge(S["top_set"], after(b, d))
                    V.tensor_scalar(ntop[:, :], top[:, 0:1], -1.0, None, ALU.mult).then_inc(S["ntop_set"], 1)
                    V.match_replace(rest, top[:, :], logit, -3.0e38).then_inc(S["rest_set"], 1)
                    dve.wait_ge(S["rest_set"], after(b, d))
                    V.tensor_tensor(chosen[:, :], logit, rest, ALU.not_equal).then_inc(S["sel_set"], 1)
                if g == 2 and live(b, -2) and not last_batches(b):
                    expert_weights(b)
                if isinstance(b, int) and b == 0:
                    statistics(g + 1)
                if g == 3 and live(b, -2) and not last_batches(b):
                    send_rows(b)
                d = -1
                if g == 3 and live(b, d):
                    dve.wait_ge(S["rstd2_set"], after(b, d))
                    need(dve, S["srow_set"], at(b, d))
                    V.tensor_scalar(xrow[:, 0:D], xall[:, bass.ds(at(b, d), 1), :].rearrange("p b d -> p (b d)"),
                                    mv2[:, 0:1], rstd2[:, :], ALU.subtract, ALU.mult).then_inc(S["xrow_set"], 1)
                if g == 3 and live(b, 1):
                    dve.wait_ge(S["qk_mm"], after(b, 1))
                    dve.wait_ge(S["k_ev"], after(b, 1))
                    k0 = m4[:, 1, LAT:P]
                    V.tensor_tensor(ktok[:, LAT:P], k0, const("cos"), ALU.mult)
                    V.tensor_tensor(kropet[:, 0:HALF], k0[:, HALF:ROT], const("sin")[:, 0:HALF], ALU.mult)
                    V.tensor_tensor(kropet[:, HALF:ROT], k0[:, 0:HALF], const("sin")[:, HALF:ROT], ALU.mult).then_inc(S["krope_b"], 1)
                    dve.wait_ge(S["krope_b"], after(b, 1))
                    V.tensor_tensor(ktok[:, LAT:P], ktok[:, LAT:P], kropet, ALU.add).then_inc(S["ktok_set"], 1)

            schedule(dve, step)

            dve.wait_ge(S["map_mm"], 1)
            V.tensor_tensor(cnt[:, :], pM[0:NE, 0:1].to_broadcast([NE, 16]), const("thr")[0:NE, :], ALU.is_gt).then_inc(S["map_s"], 1)
            V.tensor_copy(cum[:, 1, :], pM[:, 128:128 + NE]).then_inc(S["map_s"], 1)
            dve.wait_ge(S["map_s"], 2)
            V.reduce_sum(ntile[:, :], cnt[:, :], AX.X).then_inc(S["map_s"], 1)
            dve.wait_ge(S["map_s"], 3)
            V.tensor_copy(ntileb[:, :], ntile[:, :].to_broadcast([NE, P])).then_inc(S["map_s"], 1)
            dve.wait_ge(S["map_mm"], 2)
            V.tensor_copy(cum[:, 0, :], pM[:, 256:256 + NE]).then_inc(S["map_s"], 1)
            dve.wait_ge(S["map_s"], 5)
            k = [5]

            def link(ins):
                k[0] += 1
                ins.then_inc(S["map_s"], 1)
                dve.wait_ge(S["map_s"], k[0])

            tile3 = const("tile").unsqueeze(2).to_broadcast([P, 2, NE])
            cum3 = cum[:, 0, :].unsqueeze(1).to_broadcast([P, 2, NE])
            n3 = cum[:, 1, :].unsqueeze(1).to_broadcast([P, 2, NE])
            link(V.tensor_tensor(cmp_[:, :, :], tile3, cum3, ALU.is_ge))
            link(V.reduce_sum(tmap[:, 0, :], cmp_[:, :, :], AX.X))
            link(V.tensor_tensor(cmpc[:, :, :], cmp_[:, :, :], cum3, ALU.mult))
            link(V.tensor_reduce(tmap[:, 1, :], cmpc[:, :, :], AX.X, ALU.max))
            link(V.tensor_scalar(tmap[:, 2, :], tmap[:, 0, :], float(TPE), 1.0, ALU.mult, ALU.add))
            link(V.tensor_tensor(cmp_[:, :, :], tmap[:, 2, :].unsqueeze(2).to_broadcast([P, 2, NE]),
                                 const("base1").unsqueeze(1).to_broadcast([P, 2, NE]), ALU.is_equal))
            link(V.tensor_tensor(cmpc[:, :, :], cmp_[:, :, :], n3, ALU.mult))
            link(V.reduce_sum(tmap[:, 3, :], cmpc[:, :, :], AX.X))
            link(V.tensor_tensor(tmap[:, 4, :], const("tile"), tmap[:, 1, :], ALU.subtract))
            link(V.tensor_scalar(tmap[:, 4, :], tmap[:, 4, :], float(P), None, ALU.mult))
            link(V.tensor_scalar(tmap[:, 5, :], tmap[:, 3, :], -float(P), 0.0, ALU.add, ALU.max))
            link(V.tensor_tensor(tmap[:, 5, :], tmap[:, 5, :], tmap[:, 4, :], ALU.min))
            link(V.tensor_tensor(tmap[:, 6, :], tmap[:, 4, :], tmap[:, 5, :], ALU.subtract))
            link(V.tensor_scalar(tmap[:, 7, :], tmap[:, 0, :], float(TPE), None, ALU.mult))
            link(V.tensor_tensor(tmap[:, 8, :], tmap[:, 7, :], tmap[:, 5, :], ALU.add))
            link(V.tensor_scalar(tmap[:, 8, :], tmap[:, 8, :], float(SPARE), None, ALU.min))
            link(V.tensor_scalar(tmap[:, 9, :], tmap[:, 0, :], float(NE - 1), None, ALU.min))
            for c in range(2):
                for m, r in enumerate((9, 8, 6)):
                    last = V.tensor_scalar(diag[:, c, m, :], const("ident"), tmap[:, r, c:c + 1], None, ALU.mult)
                last.then_inc(S["tab_diag"], 1)
            for c in range(2):
                dve.wait_ge(S["map_mm"], c + 3)
                V.tensor_copy(tabf[:, :, c, :], (pM, pQ)[c][:, 0:3 * P].rearrange("p (m a) -> p m a", m=3)).then_inc(S["tab_ev"], 1)
            dve.wait_ge(S["tab_ev"], 2)
            tabr = tabf[0:1, :, :, :].rearrange("p m a c -> p m (a c)")
            V.memset(tabi[0:1, 0, 0:2], 0)
            V.tensor_copy(tabi[0:1, 0, 2:NT + 2], tabr[:, 0, 0:NT])
            V.tensor_copy(tabi[0:1, 1, 0:NT], tabr[:, 1, 0:NT]).then_inc(S["tab_all"], 1)
            dumpc = const("dump").unsqueeze(2).to_broadcast([P, 2, P])
            link(V.tensor_tensor(valid[:, :, :], const("tok").unsqueeze(2).to_broadcast([P, 2, P]), tabf[:, 2, :, :], ALU.is_ge))
            link(V.tensor_tensor(dumpt[:, :, :], valid[:, :, :], dumpc, ALU.mult))
            link(V.tensor_tensor(dumpt[:, :, :], dumpc, dumpt[:, :, :], ALU.subtract))
            V.sem_inc(S["tab_all"], 1)

            validr = valid[:, :, :].rearrange("p a c -> p (a c)")
            dumpr = dumpt[:, :, :].rearrange("p a c -> p (a c)")

            held = {}

            def slot(n, j):
                if (t := tile_at(n, j, 0)) is not None:
                    p = t % NCH
                    if j == 0:
                        held["expert"] = entries(dve, 0, n * UNROLL + 2, UNROLL, NE - 1)
                    dve.wait_ge(S["silu_set"][p], tile_done(n, t))
                    if not early_tile(n, t - NCH):
                        dve.wait_ge(S["yt_set"][p], tile_done(n, t - NCH))
                    V.tensor_copy(idf[:, p:p + 1], xt[:, t % XB, IDC:IDC + 1])
                    V.scalar_tensor_tensor(hid[:, p % 2], act_[:, p % 2], xt[:, t % XB, bass.ds(held["expert"][t] + D, 1)],
                                           (pE, pS)[p % 2][:, FF:2 * FF], ALU.mult, ALU.mult).then_inc(S["hid_set"][p], 1)
                if (t := tile_at(n, j, 2)) is not None:
                    p = t % NCH
                    if not early_tile(n, t - NCH):
                        dve.wait_ge(added[(t - NCH) % ACCS], addition_done(n, t - NCH))
                    i = bass.ds(n * UNROLL + t, 1)
                    V.tensor_scalar(idt[:, p:p + 1], idf[:, p:p + 1], validr[:, i], dumpr[:, i], ALU.mult, ALU.add)
                    dve.wait_ge(S["dn_mm"][p], tile_done(n, t))
                    V.tensor_copy(yt[:, p, :], (pY, pM)[p % 2][:, 0:D]).then_inc(S["yt_set"][p], 1)

            slots_of(dve, slot)
            for h, (b0, b1) in enumerate(SUMS):
                dve.wait_ge(acc_ld[h], ACCS * 16)
                for j in range(ACCS):
                    xh = xall[:, b0:b1, :]
                    V.tensor_tensor(xh, xh, accb[:, j, b0:b1, :], ALU.add).then_inc(S["fin_set"], 1)
                    dve.wait_ge(S["fin_set"], h * ACCS + j + 1)

        @block.tensor
        def _(pe):
            T = nc.tensor
            ident = const("ident")

            def transpose_inputs(b):
                pe.wait_ge(S["xn_set"], after(b, 1))
                pe.wait_ge(S["ld_ctx"], after(b, 1) * 16)
                need(pe, S["kT_ev"], at(b, 1))
                for k in range(DK):
                    T.transpose(m4[:, k, :], xn[:, k * P:k * P + P], ident)
                for k in range(DK):
                    last = T.transpose(m4[:, 2 + k, :], ctxb[:, k * P:k * P + P], ident)
                last.then_inc(S["inT_mm"], 1)

            pe.wait_ge(S["ld_const"], 16)
            transpose_inputs(-1)
            pe.wait_ge(S["ld_w1"], 4 * 16)
            for h in range(NG):
                for a in range(GH):
                    last = T.matmul((pQ, pT, pE, pS)[h][0:QC, a * LAT:a * LAT + LAT], wuqT[:, h * GH + a, :], wukT[:, h * GH + a, :],
                                    start=True, stop=True)
                last.then_inc(S["fold_mm"], 1)
            for k in range(DK):
                last = T.matmul(pY[:, k * ROT:k * ROT + ROT], wkvcT[:, k * P:k * P + P], wkr, start=True, stop=True)
            last.then_inc(S["fold_mm"], 1)
            pe.wait_ge(S["fold_ev"], NG + 1)
            pe.wait_ge(S["ld_w2"], 4 * 16)
            pe.wait_ge(S["casts"], NCASTS)

            def step(b, g):
                if cur := group(b, g, 3):
                    d, gg = cur
                    pe.wait_ge(S["eT_ev"][gg], after(b, d))
                    pe.wait_ge(S["kval_set"], after(b, d))
                    for a in range(2):
                        last = T.matmul(z2[a * LAT:a * LAT + LAT, :, :], kval, eT[:, gg % 2, a::2, :], start=True, stop=True)
                    last.then_inc(S["z_mm"][gg], 1)
                if cur := group(b, g, 0):
                    d, gg = cur
                    pe.wait_ge(S["qc_ev"], after(b, d))
                    T.matmul(pQ[:, :], qcT, wq[:, gg * GH:gg * GH + GH, :].rearrange("p h c -> p (h c)"),
                             start=True, stop=True).then_inc(S["q_mm"][gg], 1)
                if g == 2 and live(b, -2):
                    pe.wait_ge(S["sel_set"], after(b, -2))
                    T.matmul(ranks, trib[:, :], chosen[:, :], start=True, stop=False)
                    T.matmul(ranks, onesb[:, :], before[:, :], start=False, stop=True).then_inc(S["rank_mm"], 1)
                if cur := group(b, g, 1):
                    d, gg = cur
                    pe.wait_ge(S["qT_ev"][gg], after(b, d))
                    pe.wait_ge(S["kT_ev"], after(b, d))
                    pe.wait_ge(S["bias_set"], after(b, d))
                    T.matmul(pS[:, :], identb[:, :], bias[:, :].unsqueeze(1).to_broadcast([P, GH, P]), start=True, stop=True)
                    for a in range(GH):
                        last = T.matmul(s4[:, a, :], qT[:, gg % 2, a, :], kT, start=False, stop=True, skip_group_check=True)
                    last.then_inc(S["s_mm"][gg], 1)
                if folds(b, g):
                    n = g
                    if n == 0:
                        pe.wait_ge(S["ld_w3"], 2 * 16)
                    else:
                        pe.wait_ge(S["fold2_ev"], n)
                    for m in range(2):
                        for a in range(2):
                            last = T.matmul(pY[a * LAT:a * LAT + LAT, m * D:m * D + D], wuvT[:, 4 * n + 2 * m + a, :],
                                            wo[:, 4 * n + 2 * m + a, :], start=True, stop=True)
                    last.then_inc(S["fold2_mm"], 1)
                if g == 0 and live(b, 0):
                    pe.wait_ge(S["ktok_set"], after(b, 0))
                    T.transpose(m4[:, 0, :], ktok, ident).then_inc(S["kT_mm"], 1)
                if cur := group(b, g, 2):
                    d, gg = cur
                    pe.wait_ge(S["norm_set"][gg], after(b, d))
                    for a in range(GH):
                        last = T.transpose(e4[:, a, :], ex[:, gg % 2, a, :], ident)
                    last.then_inc(S["eT_mm"][gg], 1)
                if g == 0 and live(b, -2):
                    pe.wait_ge(S["xrow_set"], after(b, -2))
                    for k in range(DK):
                        last = T.transpose(rowT[:, k, :], xrow[:, k * P:k * P + P], ident)
                    last.then_inc(S["x2T_mm"], 1)
                if g == 1 and live(b, -2):
                    pe.wait_ge(S["x2T_ev"], after(b, -2))
                    for k in range(DK):
                        last = T.matmul(logits, x2T[:, k, :], wrt[:, k, :], start=(k == 0), stop=(k == DK - 1))
                    last.then_inc(S["lg_mm"], 1)
                if g == 3 and live(b, 1):
                    pe.wait_ge(S["inT_ev"], after(b, 1))
                    for k in range(DK):
                        T.matmul(m4[0:QC, 0, :], wdq[:, k, :], xcT[:, k, :], start=(k == 0), stop=(k == DK - 1))
                    for k in range(DK):
                        last = T.matmul(m4[:, 1, :], xcT[:, 2 + k, :], wk[:, k, :], start=(k == 0), stop=(k == DK - 1))
                    last.then_inc(S["qk_mm"], 1)
                if cur := group(b, g, 3):
                    d, gg = cur
                    pe.wait_ge(S["zT_ev"][gg], after(b, d))
                    if gg == 0:
                        need(pe, S["x2_set"], at(b, d))
                    if isinstance(b, int) and b == 0 and gg == 0:
                        pe.wait_ge(S["fold2_ev"], FOLDS)
                    for k in range(2):
                        last = T.matmul(pY[:, 0:D], zT[:, gg % 2, k, :], wc[:, gg * 2 + k, :],
                                        start=(gg == 0 and k == 0), stop=(gg == NG - 1 and k == 1))
                    if gg == NG - 1:
                        last.then_inc(S["y_mm"], 1)
                if cur := group(b, g, 0):
                    d, gg = cur
                    pe.wait_ge(S["q_lat"][gg], after(b, d))
                    pe.wait_ge(S["rope_set"][gg], after(b, d))
                    for a in range(GH):
                        last = T.transpose(t4[:, a, :], qs[:, gg % 2, a, :], ident)
                    last.then_inc(S["qT_mm"][gg], 1)
                if g == 2 and live(b, 1) and live(b, 0):
                    transpose_inputs(b)

            schedule(pe, step)

            pe.wait_ge(S["before_set"], NB + 1)
            pe.wait_ge(S["place_set"], NB)
            T.matmul(pM[0:NE, 0:1], before[:, :], onesb[:, 0:1], start=True, stop=True)
            T.matmul(pM[:, 128:128 + NE], onesb[:, :], before[:, :], start=True, stop=True).then_inc(S["map_mm"], 1)
            pe.wait_ge(S["map_s"], 4)
            T.matmul(pM[:, 256:256 + NE], ntileb[:, :], uptob[0:NE, :], start=True, stop=True).then_inc(S["map_mm"], 1)
            pe.wait_ge(S["map_s"], 5)
            for c in range(2):
                pe.wait_ge(S["tab_diag"], c + 1)
                T.matmul((pM, pQ)[c][:, 0:3 * P], onesf[:, :], diag[:, c].rearrange("p m a -> p (m a)"),
                         start=True, stop=True).then_inc(S["map_mm"], 1)
            pe.wait_ge(S["tab_ev"], 2)
            pe.wait_ge(S["tab_all"], 2)
            pe.wait_ge(S["ld_gu"], NE // 4 * 16)

            held = {}

            def slot(n, j):
                if j == 0:
                    held["expert"] = entries(pe, 0, n * UNROLL, UNROLL + 2, NE - 1)
                if (t := tile_at(n, j, -1)) is not None:
                    p = t % NCH
                    pe.wait_ge(xt_ld[t % XB], rows_loaded(n, t))
                    for k in range(DK):
                        last = T.transpose((pQ, pT)[p % 2][:, k * P:k * P + P], xt[:, t % XB, k * P:k * P + P], ident)
                    last.then_inc(S["xtT_mm"][p], 1)
                if (t := tile_at(n, j, 0)) is not None:
                    p = t % NCH
                    e = held["expert"][t + 2]
                    pe.wait_ge(S["xtT_ev"][p], tile_done(n, t))
                    for k in range(DK):
                        last = T.matmul((pE, pS)[p % 2][:, 0:2 * FF], xtT[:, p % 2, k, :],
                                        wgu[:, bass.ds(e, 1), k, :].rearrange("p e f -> p (e f)"), start=(k == 0), stop=(k == DK - 1))
                    last.then_inc(S["gu_mm"][p], 1)
                if (t := tile_at(n, j, 1)) is not None:
                    p = t % NCH
                    pe.wait_ge(S["hid_set"][p], tile_done(n, t))
                    T.transpose((pZ, pR)[p % 2][0:FF, 0:P], hid[:, p % 2], ident).then_inc(S["hT_mm"][p], 1)
                if (t := tile_at(n, j, 2)) is not None:
                    p = t % NCH
                    e = held["expert"][t + 2]
                    if isinstance(n, int) and n * UNROLL + t == 0:
                        pe.wait_ge(S["ld_down"], (NG + 1 + 8 + 1) * 16)
                    pe.wait_ge(S["hT_ev"][p], tile_done(n, t))
                    if isinstance(n, int) and n * UNROLL + t == NT - 1:
                        pe.wait_ge(S["yt_set"][(t - 2) % NCH], tile_done(n, t - 2))
                    T.matmul((pY, pM)[p % 2][:, 0:D], hidT[:, p % 2], wdn[0:FF, bass.ds(e, 1), :].rearrange("p e d -> p (e d)"),
                             start=True, stop=True).then_inc(S["dn_mm"][p], 1)

            slots_of(pe, slot)


def table():
    import numpy as np
    c = np.zeros((P, NCONST), np.float32)
    p = np.arange(P)
    half = np.arange(HALF, dtype=np.float32) / HALF
    angle = p[:, None].astype(np.float32) * (1.0 / np.float32(10000.0) ** half).astype(np.float32)
    cos, sin = np.cos(angle), np.sin(angle)
    e = np.arange(NE)
    parts = {"ident": np.eye(P), "tri": p[:, None] < p[None, :], "cos": np.concatenate([cos, cos], 1),
             "sin": np.concatenate([-sin, sin], 1), "kidx": np.tile(p, (P, 1)), "base1": np.tile(e * TPE + 1, (P, 1)),
             "upto": p[:, None] <= e[None, :], "tile": np.stack([p, p + P], 1), "dump": NTOK + p[:, None], "tok": p[:, None],
             "thr": np.tile(np.arange(16) * P, (P, 1))}
    for n, v in parts.items():
        c[:, COL[n][0]:COL[n][1]] = v
    return c


def kernel(**inputs):
    import numpy as np
    import concourse.bacc as bacc
    from concourse.bass_utils import run_bass_kernel_spmd as run

    def w(name):
        return np.ascontiguousarray(inputs[name])

    pre, ffn = "L0_xattn_W_", "L0_ffn_W_"
    arrays = {
        "x": w("x"),
        "ctx": w("ctx_2048"),
        "seg": w("itok_BxS_0_1023").T,
        "consts": table(),
        "w_kvc": w(pre + "kvc").reshape(DK, P, LAT).transpose(1, 0, 2),
        "w_kvc_t": w(pre + "kvc").T,
        "w_dq": w(pre + "dq").reshape(DK, P, QC).transpose(1, 0, 2),
        "w_uq_t": w(pre + "uq").reshape(QC, NH, HD).transpose(2, 1, 0),
        "w_qr": w(pre + "qr").reshape(QC, NH, ROT),
        "w_uk_t": w(pre + "uk").reshape(LAT, NH, HD).transpose(2, 1, 0),
        "w_kr": w(pre + "kr"),
        "w_uv_t": w(pre + "uv").reshape(LAT, NH, HD).transpose(2, 1, 0),
        "w_o": w(pre + "o").reshape(NH, HD, D).transpose(1, 0, 2),
        "w_router": w(ffn + "router").reshape(DK, P, NE).transpose(1, 0, 2),
        "w_gu": np.concatenate([w(ffn + "gate"), w(ffn + "up")], axis=2).reshape(NE, DK, P, 2 * FF).transpose(2, 0, 1, 3),
        "w_down": w(ffn + "down").transpose(1, 0, 2),
    }
    nc = bacc.Bacc("TRN2", target_bir_lowering=False, num_devices=1)
    given, args = {}, []
    for name, a in arrays.items():
        a = np.ascontiguousarray(a)
        given["in_" + name] = a
        args.append(nc.dram_tensor("in_" + name, a.shape, mybir.dt.from_np(a.dtype), kind="ExternalInput").ap())
    args.append(nc.dram_tensor("out_0", (NB, P, D), F32, kind="ExternalOutput").ap())
    build(nc, *args)
    r = run(nc, [given], core_ids=[0])
    return r.results[0]["out_0"]
```
